# Optimizing a Trainium2 kernel written in Bass

```python
import numpy as np
import jax
import jax.numpy as jnp

def _softmax(x, axis=-1):
    return jax.nn.softmax(x, axis=axis)

def _gelu(x):
    return jax.nn.gelu(x, approximate=True)

def _silu(x):
    return jax.nn.silu(x)

def _sigmoid(x):
    return jax.nn.sigmoid(x)

def _layernorm(x, axis=-1, eps=1e-05):
    m = jnp.mean(x, axis=axis, keepdims=True)
    v = jnp.var(x, axis=axis, keepdims=True)
    return (x - m) / jnp.sqrt(v + eps)

def _scatter_add(tgt, idx, src, axis=0):
    return tgt.at[idx].add(src)

def _segment_sum(src, seg, n):
    return jax.ops.segment_sum(src, seg, n)
kernel_name = 'mk_adj_resnorm_d2_adj_r2_710379'

def setup_inputs(seed: int=0):
    np.random.seed(seed)
    _w = jnp.asarray

    def _rec_inputs():
        import jax
        import jax.numpy as jnp
        _gk = jax.random.key(seed)
        x = -0.0005207 + 1.001 * jax.random.normal(jax.random.fold_in(_gk, 1), (4096, 128), jnp.float32)
        _a = jax.random.bernoulli(jax.random.fold_in(_gk, 2), 0.000488281, (4096, 4096))
        _a = jnp.logical_or(_a, jnp.swapaxes(_a, -1, -2))
        _a = jnp.logical_or(_a, jnp.eye(4096, dtype=bool))
        _af = _a.astype(jnp.float32)
        _af = _af * jax.random.uniform(jax.random.fold_in(_gk, 3), (4096, 4096), jnp.float32, 0.05, 1)
        adj = _af
        return (x, adj)
    x, adj = _rec_inputs()

    def _L0_gnn_setup():
        import jax, jax.numpy as jnp
        import numpy as np
        N = 4096
        D = 128
        L = 3

        def _cxin_conv(x, a, eps, W, b):
            ax = a @ x
            h = ax + (1.0 + eps[0]) * ax
            for i in range(L):
                h = jax.nn.relu(h @ W[i].T + b[i])
            return h
        key = jax.random.key(seed)
        ks = jax.random.split(key, 8)
        s = 1.0 / np.sqrt(D)
        return {'x1': jax.random.normal(ks[0], (N, D), jnp.float32), 'x2': jax.random.normal(ks[1], (N, D), jnp.float32), 'G1': jax.random.uniform(ks[2], (N, N), jnp.float32), 'G2': jax.random.uniform(ks[3], (N, N), jnp.float32), 'eps1': jnp.zeros((1,), jnp.float32), 'eps2': jnp.zeros((1,), jnp.float32), 'W1': jax.random.normal(ks[4], (L, D, D), jnp.float32) * s, 'b1': jnp.zeros((L, D), jnp.float32), 'W2': jax.random.normal(ks[5], (L, D, D), jnp.float32) * s, 'b2': jnp.zeros((L, D), jnp.float32), 'Wm': jax.random.normal(ks[6], (D, 2 * D), jnp.float32) * (1.0 / np.sqrt(2 * D)), 'bm': jnp.zeros((D,), jnp.float32)}
    _L0_gnn_all = _L0_gnn_setup()
    _L0_gnn_in = {k: v for k, v in _L0_gnn_all.items() if k in ('x2', 'eps1', 'eps2', 'W1', 'b1', 'W2', 'b2', 'Wm', 'bm')}
    del _L0_gnn_all

    def _L1_gnn_setup():
        import jax, jax.numpy as jnp
        import numpy as np
        N, F_IN, F_OUT = (4096, 128, 128)
        key = jax.random.key(seed)
        k1, k2, k3, k4 = jax.random.split(key, 4)
        X = jax.random.normal(k1, (N, F_IN), dtype=jnp.float32)
        A = jax.random.uniform(k2, (N, N), dtype=jnp.float32)
        W = jax.random.normal(k3, (F_OUT, F_IN), dtype=jnp.float32) * (1.0 / np.sqrt(F_IN))
        b = jax.random.normal(k4, (F_OUT,), dtype=jnp.float32) * 0.01
        return {'X': X, 'A': A, 'W': W, 'b': b}
    _L1_gnn_all = _L1_gnn_setup()
    _L1_gnn_in = {k: v for k, v in _L1_gnn_all.items() if k in ('W', 'b')}
    del _L1_gnn_all
    return {'x': x, 'adj': adj, 'L0_gnn_x2': _L0_gnn_in['x2'], 'L0_gnn_eps1': _L0_gnn_in['eps1'], 'L0_gnn_eps2': _L0_gnn_in['eps2'], 'L0_gnn_W1': _L0_gnn_in['W1'], 'L0_gnn_b1': _L0_gnn_in['b1'], 'L0_gnn_W2': _L0_gnn_in['W2'], 'L0_gnn_b2': _L0_gnn_in['b2'], 'L0_gnn_Wm': _L0_gnn_in['Wm'], 'L0_gnn_bm': _L0_gnn_in['bm'], 'L1_gnn_W': _L1_gnn_in['W'], 'L1_gnn_b': _L1_gnn_in['b']}

def reference(x, adj, L0_gnn_x2, L0_gnn_eps1, L0_gnn_eps2, L0_gnn_W1, L0_gnn_b1, L0_gnn_W2, L0_gnn_b2, L0_gnn_Wm, L0_gnn_bm, L1_gnn_W, L1_gnn_b):
    import jax
    import jax.numpy as jnp

    def _L0_gnn_ref(x1, x2, G1, G2, eps1, eps2, W1, b1, W2, b2, Wm, bm):
        import jax, jax.numpy as jnp
        import numpy as np
        N = 4096
        D = 128
        L = 3

        def _cxin_conv(x, a, eps, W, b):
            ax = a @ x
            h = ax + (1.0 + eps[0]) * ax
            for i in range(L):
                h = jax.nn.relu(h @ W[i].T + b[i])
            return h
        out1 = _cxin_conv(x1, G1, eps1, W1, b1)
        out2 = _cxin_conv(x2, G2, eps2, W2, b2)
        merged = jnp.concatenate((out1, out2), axis=1)
        return merged @ Wm.T + bm

    def _L1_gnn_ref(X, A, W, b):
        import jax, jax.numpy as jnp
        import numpy as np
        N, F_IN, F_OUT = (4096, 128, 128)
        A_hat = A + jnp.eye(A.shape[0], dtype=A.dtype)
        deg = jnp.sum(A_hat, axis=1)
        d = jnp.where(deg > 0, jax.lax.rsqrt(deg), 0.0)
        A_norm = d[:, None] * A_hat * d[None, :]
        out = A_norm @ X
        out = out @ W.T + b
        return out
    x = _layernorm(x + _L0_gnn_ref(x, L0_gnn_x2, adj, adj, L0_gnn_eps1, L0_gnn_eps2, L0_gnn_W1, L0_gnn_b1, L0_gnn_W2, L0_gnn_b2, L0_gnn_Wm, L0_gnn_bm), axis=-1)
    x = _layernorm(x + _L1_gnn_ref(x, adj, L1_gnn_W, L1_gnn_b), axis=-1)
    return x

_drawn_inputs = setup_inputs


def setup_inputs(seed=0):
    import zlib

    import numpy as np

    out = dict(_drawn_inputs(seed))
    spreads = {'L0_gnn_b1': (0.0, 0.1), 'L0_gnn_b2': (0.0, 0.1), 'L0_gnn_bm': (0.0, 0.1)}
    factors = {'L1_gnn_b': 6.937}
    for name, (base, spread) in spreads.items():
        noise = np.random.default_rng([zlib.crc32(name.encode()), seed]).standard_normal(out[name].shape)
        drawn = base * np.exp(spread * noise) if base else spread * noise
        out[name] = jnp.asarray(drawn.astype(out[name].dtype))
    for name, factor in factors.items():
        out[name] = (out[name] * factor).astype(out[name].dtype)
    return out
```

```python
from contextlib import ExitStack

import concourse.bass as bass
from concourse import mybir

F32 = mybir.dt.float32
F32R = mybir.dt.float32r
ALU = mybir.AluOpType
ACT = mybir.ActivationFunctionType

P = 128
N = 4096
QUARTERS = 4
QW = N // QUARTERS
KB = QW // P
JB = N // P
PAIRS = JB // 2
CW = 512
CH = QW // CW
M = 2 * CH
LAYERS = 3
RAW = 4
SPLIT = 4
LN_EPS = 1e-5
TINY = 1.1754944e-38

W1_AT = 0
W2_AT = W1_AT + LAYERS * P
WM_AT = W2_AT + LAYERS * P
WO_AT = WM_AT + 2 * P
BM_AT = WO_AT + P
BO_AT = BM_AT + P
B1_AT = BO_AT + P
B2_AT = B1_AT + LAYERS
EPS_AT = B2_AT + LAYERS
PARAMS = EPS_AT + 2

PE_DENSE = {2: 0, 5: 1, 8: 2}
PE_MERGE = 11
PE_PROJECT = 3
PE_ADD_Y = 28
ACT_EVACUATE = 2
ACT_RELU = {k + SPLIT + 1: l for k, l in PE_DENSE.items()}
DVE_RESIDUAL = PE_MERGE + SPLIT + 1
ACT_NORM = 24
DVE_RESIDUAL2 = PE_PROJECT + SPLIT + 1
ACT_NORM2 = 20


def build(nc, a_t, x1, x2, params, out):
    with ExitStack() as ctx:
        def sb(name, shape, dt=F32):
            return ctx.enter_context(nc.sbuf_tensor(name, shape, dt))

        def sem(name):
            return ctx.enter_context(nc.semaphore(name))

        x1hi = sb("x1hi", [P, QUARTERS, QW], F32R)
        x1lo = sb("x1lo", [P, QUARTERS, QW], F32R)
        x2hi = sb("x2hi", [P, QUARTERS, QW], F32R)
        x2lo = sb("x2lo", [P, QUARTERS, QW], F32R)
        xn = sb("xn", [P, QUARTERS, QW])
        raw = sb("raw", [P, RAW, 2, QW])
        ahi = sb("ahi", [P, SPLIT, QW], F32R)
        alo = sb("alo", [P, SPLIT, QW], F32R)
        h = sb("h", [P, M, CW])
        rowsum = sb("rowsum", [P, QW])
        rowsum_all = sb("rowsum_all", [P, QW])
        xb = sb("xb", [P, KB, P])
        z = sb("z", [P, KB, P])
        yt = sb("yt", [P, KB, P])
        ydhi = sb("ydhi", [P, QW], F32R)
        ydlo = sb("ydlo", [P, QW], F32R)
        outn = sb("outn", [P, QW])
        par = sb("par", [P, PARAMS])
        gain = sb("gain", [P, 2])
        ones = sb("ones", [P, 1])
        ident = sb("ident", [P, P])
        identr = sb("identr", [P, P], F32R)
        halves = sb("halves", [P, KB])
        epsilons = sb("epsilons", [P, KB])
        minus = sb("minus", [P, KB])
        stats = sb("stats", [P, KB, 6])
        mv = sb("mv", [P, KB, 2])
        vareps = sb("vareps", [P, KB])
        rstd = sb("rstd", [P, KB])
        shift = sb("shift", [P, KB])
        nshift = sb("nshift", [P, KB])
        degc = sb("degc", [P, KB])
        degpos = sb("degpos", [P, KB])
        degpow = sb("degpow", [P, KB])
        dall = sb("dall", [P, QUARTERS, KB])
        dcur = sb("dcur", [P, KB])
        ps = [ctx.enter_context(nc.psum_tensor(f"ps{i}", [P, CW], F32)) for i in range(M)]
        pd = ctx.enter_context(nc.psum_tensor("pd", [P, M, CW], F32))
        merged = pd[:, 0:2, :].rearrange("p c (k d) -> p (c k) d", d=P)
        degree = pd[:, 2, 0:KB]

        params_in = sem("params_in")
        x_in = [sem(f"x_in{i}") for i in range(4)]
        raw_in = [sem(f"raw_in{i}") for i in range(RAW)]
        x_hi = sem("x_hi")
        x_split = sem("x_split")
        hi_ready = sem("hi_ready")
        lo_ready = sem("lo_ready")
        rowsum_step = sem("rowsum_step")
        raw_used = sem("raw_used")
        block_used = sem("block_used")
        ax_done = sem("ax_done")
        h_ready = sem("h_ready")
        dense_done = sem("dense_done")
        merge_done = sem("merge_done")
        xb_step = sem("xb_step")
        xb_ready = sem("xb_ready")
        deg_ready = sem("deg_ready")
        z_ready = sem("z_ready")
        stats_step = sem("stats_step")
        stats_ready = sem("stats_ready")
        norm_step = sem("norm_step")
        norm_ready = sem("norm_ready")
        xn_ready = sem("xn_ready")
        y_step = sem("y_step")
        y_step2 = sem("y_step2")
        y_part = sem("y_part")
        y_ready = sem("y_ready")
        yd_ready = sem("yd_ready")
        yd_added = sem("yd_added")
        ay_done = sem("ay_done")
        ay_copied = sem("ay_copied")
        project_done = sem("project_done")
        out_ready = sem("out_ready")
        out_written = sem("out_written")
        const_step = sem("const_step")
        const_ready = sem("const_ready")
        gain_ready = sem("gain_ready")

        def wait(eng, s, value):
            if not isinstance(value, int) or value > 0:
                eng.wait_ge(s, value)

        X_PIECES = 2 * QUARTERS
        x_dram = (x1, x2)
        x_hi_parts = (x1hi, x2hi)
        x_lo_parts = (x1lo, x2lo)
        as_f32 = lambda ap: ap.bitcast(F32)
        block_of = lambda t, j: t[:, j // KB, (j % KB) * P:(j % KB + 1) * P]

        block = ctx.enter_context(nc.Block())

        @block.sync
        def _(sp):
            def load_x(i):
                if i >= 4:
                    sp.wait_ge(x_split, i - 3)
                sp.dma_start(xn[:, i % 4, :], x_dram[i % 2][i // 2]).then_inc(x_in[i % 4], 16)

            load_x(0)
            load_x(1)
            for p in range(RAW):
                sp.dma_start(raw[:, p], a_t[p]).then_inc(raw_in[p], 16)
                if p == 0:
                    sp.dma_start(par[:, :], params).then_inc(params_in, 16)
                if p == 1:
                    load_x(2)
                    load_x(3)
            for i in range(4, X_PIECES):
                load_x(i)
            with sp.Fori(1, QUARTERS * PAIRS // RAW) as g:
                for s in range(RAW):
                    sp.wait_ge(raw_used, g * RAW + (s + 1 - RAW))
                    sp.dma_start(raw[:, s], a_t[bass.ds(g * RAW + s, 1)]
                                 .rearrange("o p t i -> (o p) t i")).then_inc(raw_in[s], 16)
            for s in range(RAW):
                sp.wait_ge(raw_used, QUARTERS * PAIRS + s + 1 - RAW)
                sp.dma_start(raw[:, s], a_t[s]).then_inc(raw_in[s], 16)
            with sp.Fori(1, QUARTERS * PAIRS // RAW) as g:
                for s in range(RAW):
                    sp.wait_ge(lo_ready, g * (2 * RAW) + (QUARTERS * JB + 2 * (s + 1 - RAW)))
                    sp.dma_start(raw[:, s], a_t[bass.ds(g * RAW + s, 1)]
                                 .rearrange("o p t i -> (o p) t i")).then_inc(raw_in[s], 16)

        @block.tensor
        def _(pe):
            def products(q, layer, n, stationary, first_wait):
                at = q * JB + (layer * QUARTERS * JB + n + 1)
                banks = [(b, c) for b in range(len(stationary)) for c in range(CH)]
                hi = [ahi[:, n % SPLIT, c * CW:(c + 1) * CW] for c in range(CH)]
                lo = [alo[:, n % SPLIT, c * CW:(c + 1) * CW] for c in range(CH)]
                wait(pe, hi_ready, at)
                wait(pe, lo_ready, at)
                if n in (0, JB - 1):
                    order = [(b, c, k) for b, c in banks for k in range(3)]
                else:
                    order = [(b, c, k) for b in range(len(stationary)) for k in range(3) for c in range(CH)]
                for b, c, k in order:
                    whi, wlo = stationary[b]
                    w, a = ((whi, hi), (whi, lo), (wlo, hi))[k]
                    bank = b * CH + c
                    if n == 0 and k == 0:
                        first_wait(bank)
                    mm = pe.matmul(ps[bank][:, :], block_of(w, n), a[c],
                                   start=(n == 0 and k == 0), stop=(n == JB - 1 and k == 2))
                    if n == JB - 1 and k == 2 and (b, c) != banks[-1]:
                        mm.then_inc(ay_done if layer else ax_done, 1)
                mm.then_inc(block_used, 1)

            def dense(q, l):
                for m in range(M):
                    wait(pe, h_ready, q * (4 * M) + (M * l + m + 1))
                    w = par[:, (W1_AT, W2_AT)[m // CH] + l * P:(W1_AT, W2_AT)[m // CH] + (l + 1) * P]
                    pe.matmul(pd[:, m, :], w, h[:, m, :], start=True, stop=True).then_inc(dense_done, 1)

            def merge(q):
                wait(pe, h_ready, q * (4 * M) + 4 * M)
                for k in range(KB):
                    pe.matmul(degree[:, k:k + 1], rowsum_all[:, k * P:(k + 1) * P], ones[:, :],
                              start=(k == 0), stop=(k == KB - 1), skip_group_check=True)
                for k in range(KB):
                    for b in range(2):
                        mm = pe.matmul(merged[:, k, :], h[:, CH * b + k // 4, (k % 4) * P:(k % 4 + 1) * P],
                                       par[:, WM_AT + b * P:WM_AT + (b + 1) * P],
                                       start=(k % 4 == 0 and b == 0), stop=(k % 4 == 3 and b == 1),
                                       skip_group_check=True)
                mm.then_inc(merge_done, 1)

            def mlp_step(q, n):
                if n in PE_DENSE:
                    if n == min(PE_DENSE):
                        wait(pe, raw_used, q * PAIRS + PAIRS)
                        wait(pe, z_ready, q)
                        wait(pe, deg_ready, 2 * q)
                    dense(q, PE_DENSE[n])
                if n == PE_MERGE:
                    merge(q)

            def layer0_quarter(q, before):
                def empty(bank):
                    if before is not None:
                        wait(pe, h_ready, before * (4 * M) + (bank + 1))
                for n in range(JB):
                    if before is None and n % KB == 0:
                        pe.wait_ge(x_split, 2 * (n // KB + 1))
                    products(q, 0, n, ((x1hi, x1lo), (x2hi, x2lo)), empty)
                    if before is not None:
                        mlp_step(before, n)

            def project(q):
                wait(pe, ay_copied, q * CH + CH)
                if isinstance(q, int):
                    wait(pe, z_ready, QUARTERS + q)
                else:
                    pe.wait_ge(z_ready, q + QUARTERS)
                for k in range(KB):
                    mm = pe.matmul(merged[:, k, :], h[:, k // 4, (k % 4) * P:(k % 4 + 1) * P],
                                   par[:, WO_AT:WO_AT + P], start=(k % 4 == 0), stop=(k % 4 == 3),
                                   skip_group_check=True)
                mm.then_inc(project_done, 1)

            def layer1_quarter(q, before):
                def empty(bank):
                    if before is None:
                        wait(pe, h_ready, (QUARTERS - 1) * 4 * M + bank + 1)
                    else:
                        wait(pe, ay_copied, before * CH + (bank + 1))
                for n in range(JB):
                    if before is None and n % KB == 0:
                        pe.wait_ge(y_ready, n // KB + 1)
                    products(q, 1, n, ((x1hi, x1lo),), empty)
                    if n == PE_ADD_Y:
                        wait(pe, yd_ready, q * 2 + 2)
                        for k in range(KB):
                            for part in (ydhi, ydlo):
                                mm = pe.matmul(ps[k // 4][:, (k % 4) * P:(k % 4 + 1) * P],
                                               part[:, k * P:(k + 1) * P], identr[:, :],
                                               start=False, stop=False)
                        mm.then_inc(yd_added, 1)
                    if before is None:
                        mlp_step(QUARTERS - 1, n)
                    elif n == PE_PROJECT:
                        project(before)

            pe.wait_ge(const_ready, 5)
            pe.wait_ge(params_in, 16)
            layer0_quarter(0, None)
            with pe.Fori(1, QUARTERS) as q:
                layer0_quarter(q, q - 1)
            layer1_quarter(0, None)
            with pe.Fori(1, QUARTERS) as q:
                layer1_quarter(q, q - 1)
            project(QUARTERS - 1)

        @block.scalar
        def _(act):
            def round_x(i):
                act.wait_ge(x_in[i % 4], 16 * (i // 4 + 1))
                act.activation(x_hi_parts[i % 2][:, i // 2, :], xn[:, i % 4, :], ACT.Copy).then_inc(x_hi, 1)

            def round_a(q, layer, n):
                s = (n // 2) % RAW
                if n % 2 == 0:
                    act.wait_ge(raw_in[s], q * (16 * PAIRS // RAW)
                                + 16 * (layer * QUARTERS * PAIRS // RAW + n // 2 // RAW + 1))
                wait(act, block_used, q * JB + (layer * QUARTERS * JB + n + 1 - SPLIT))
                act.activation(ahi[:, n % SPLIT, :], raw[:, s, n % 2, :], ACT.Copy).then_inc(hi_ready, 1)

            def evacuate(q):
                for m in range(M):
                    if m < M - 1:
                        wait(act, ax_done, q * (M - 1) + (m + 1))
                    else:
                        wait(act, block_used, q * JB + JB)
                    act.activation(h[:, m, :], ps[m][:, :], ACT.Identity,
                                   scale=gain[:, m // CH:m // CH + 1]).then_inc(h_ready, 1)

            def relu(q, l):
                for m in range(M):
                    wait(act, dense_done, q * (LAYERS * M) + (M * l + m + 1))
                    at = (B1_AT, B2_AT)[m // CH] + l
                    act.activation(h[:, m, :], pd[:, m, :], ACT.Relu,
                                   bias=par[:, at:at + 1]).then_inc(h_ready, 1)

            def normalise(done, dst, target, ready):
                wait(act, norm_ready, done)
                for k in range(KB):
                    i = act.activation(dst(k), z[:, k, :], ACT.Identity,
                                       scale=rstd[:, k:k + 1], bias=nshift[:, k:k + 1])
                i.then_inc(ready, 1)

            def mlp_step(q, n):
                if n == ACT_EVACUATE:
                    evacuate(q)
                if n in ACT_RELU:
                    relu(q, ACT_RELU[n])
                if n == ACT_NORM:
                    if isinstance(q, int):
                        to = lambda k: xn[:, q, k * P:(k + 1) * P]
                    else:
                        to = lambda k: xn[:, bass.ds(q, 1), k * P:(k + 1) * P].rearrange("p o d -> p (o d)")
                    normalise(q + 1, to, None, xn_ready)

            def copy_ay(q):
                for c in range(CH):
                    if c < CH - 1:
                        wait(act, ay_done, q * (CH - 1) + (c + 1))
                    else:
                        wait(act, block_used, q * JB + (QUARTERS * JB + JB))
                    act.activation(h[:, c, :], ps[c][:, :], ACT.Copy).then_inc(ay_copied, 1)

            def finish(q):
                if isinstance(q, int):
                    wait(act, out_written, 16 * q)
                else:
                    act.wait_ge(out_written, q * 16)
                normalise(q + (QUARTERS + 1), lambda k: outn[:, k * P:(k + 1) * P], None, out_ready)

            def store(q):
                wait(act, out_ready, q + 1)
                dst = out[q] if isinstance(q, int) else out[bass.ds(q, 1)].rearrange("o p f -> (o p) f")
                act.dma_start(dst, outn[:, :]).then_inc(out_written, 16)

            def layer0_quarter(q, before):
                for n in range(JB):
                    round_a(q, 0, n)
                    if before is not None:
                        mlp_step(before, n)
                    elif n in (1, 8, 16):
                        round_x(2 * (1, 8, 16).index(n) + 2)
                        round_x(2 * (1, 8, 16).index(n) + 3)

            def layer1_quarter(q, before):
                for n in range(JB):
                    round_a(q, 1, n)
                    if before is None:
                        mlp_step(QUARTERS - 1, n)
                    else:
                        if n == ACT_EVACUATE:
                            copy_ay(before)
                        if n == ACT_NORM2:
                            finish(before)
                        if n == ACT_NORM2 + 1:
                            store(before)

            round_x(0)
            round_x(1)
            layer0_quarter(0, None)
            act.wait_ge(params_in, 16)
            act.wait_ge(gain_ready, 1)
            with act.Fori(1, QUARTERS) as q:
                layer0_quarter(q, q - 1)
            layer1_quarter(0, None)
            with act.Fori(1, QUARTERS) as q:
                layer1_quarter(q, q - 1)
            copy_ay(QUARTERS - 1)
            finish(QUARTERS - 1)
            store(QUARTERS - 1)
            act.wait_ge(out_written, 16 * QUARTERS)

        @block.vector
        def _(dve):
            def split_x(i):
                dve.wait_ge(x_hi, i + 1)
                dve.tensor_tensor(x_lo_parts[i % 2][:, i // 2, :], xn[:, i % 4, :],
                                  as_f32(x_hi_parts[i % 2][:, i // 2, :]), ALU.subtract).then_inc(x_split, 1)

            def split_a(q, layer, n):
                wait(dve, hi_ready, q * JB + (layer * QUARTERS * JB + n + 1))
                dve.tensor_tensor(alo[:, n % SPLIT, :], raw[:, (n // 2) % RAW, n % 2, :],
                                  as_f32(ahi[:, n % SPLIT, :]), ALU.subtract).then_inc(lo_ready, 1)

            def sum_rows(q, n):
                tile = raw[:, (n // 2) % RAW, n % 2, :]
                if n == 1:
                    wait(dve, raw_used, q * PAIRS)
                    dve.tensor_tensor(rowsum[:, :], raw[:, 0, 0, :], tile, ALU.add).then_inc(raw_used, 1)
                elif n % 2 == 0 and n:
                    wait(dve, raw_used, q * PAIRS + n // 2)
                    dve.tensor_tensor(rowsum[:, :], rowsum[:, :], tile, ALU.add).then_inc(rowsum_step, 1)
                elif n % 2:
                    wait(dve, rowsum_step, q * (PAIRS - 1) + n // 2)
                    to = rowsum_all if n == JB - 1 else rowsum
                    dve.tensor_tensor(to[:, :], rowsum[:, :], tile, ALU.add).then_inc(raw_used, 1)

            def degrees(q):
                dve.tensor_scalar(degc[:, :], degree, 1.0, TINY, ALU.add, ALU.max).then_inc(deg_ready, 1)
                dve.tensor_scalar(degpos[:, :], degree, 1.0, 0.0, ALU.add, ALU.is_gt).then_inc(deg_ready, 1)

            def statistics(done, k):
                if k == 0:
                    wait(dve, z_ready, done)
                for i in (k, k + 1):
                    dve.bn_stats(stats[:, i, :], z[:, i, :]).then_inc(stats_step, 1)

            def statistics_taken(done):
                wait(dve, stats_step, (done - 1) * KB + KB)

            def aggregate():
                for k in range(KB):
                    i = dve.bn_aggr(mv[:, k, :], stats[:, k, :])
                i.then_inc(stats_ready, 1)

            def residual(q):
                wait(dve, merge_done, q + 1)
                wait(dve, xb_ready, q + 1)
                wait(dve, xn_ready, q)
                dve.tensor_tensor(z[:, :, :], merged, xb[:, :, :], ALU.add).then_inc(z_ready, 1)

            def mlp_step(q, n):
                if n == DVE_RESIDUAL:
                    residual(q)
                if n == DVE_RESIDUAL + 1:
                    degrees(q)
                if 0 <= n - DVE_RESIDUAL - 1 < KB // 2:
                    statistics(q + 1, 2 * (n - DVE_RESIDUAL - 1))
                if n == DVE_RESIDUAL + KB // 2 + 1:
                    aggregate()

            def residual2(q):
                wait(dve, project_done, q + 1)
                wait(dve, xb_ready, q + (QUARTERS + 1))
                if isinstance(q, int) and q == 0:
                    dve.wait_ge(xn_ready, QUARTERS)
                else:
                    wait(dve, out_ready, q)
                for k in range(KB):
                    i = dve.scalar_tensor_tensor(out=z[:, k, :], in0=merged[:, k, :], scalar=dcur[:, k:k + 1],
                                                 in1=xb[:, k, :], op0=ALU.mult, op1=ALU.add)
                i.then_inc(z_ready, 1)

            def finish_step(q, n):
                if n == DVE_RESIDUAL2:
                    residual2(q)
                if 0 <= n - DVE_RESIDUAL2 - 1 < KB // 2:
                    statistics(q + (QUARTERS + 1), 2 * (n - DVE_RESIDUAL2 - 1))
                if n == DVE_RESIDUAL2 + KB // 2 + 1:
                    aggregate()

            def layer0_quarter(q, before):
                for n in range(JB):
                    if before is not None and n == DVE_RESIDUAL + KB // 2 + 1:
                        statistics_taken(before + 1)
                    split_a(q, 0, n)
                    sum_rows(q, n)
                    if before is not None:
                        mlp_step(before, n)
                    elif n in (1, 8, 16):
                        split_x(2 * (1, 8, 16).index(n) + 2)
                        split_x(2 * (1, 8, 16).index(n) + 3)

            def layer1_quarter(q, before):
                for n in range(JB):
                    if before is None and n == DVE_RESIDUAL + KB // 2 + 1:
                        statistics_taken(QUARTERS)
                    elif before is not None and n == DVE_RESIDUAL2 + KB // 2 + 1:
                        statistics_taken(before + (QUARTERS + 1))
                    split_a(q, 1, n)
                    if before is None:
                        mlp_step(QUARTERS - 1, n)
                    else:
                        finish_step(before, n)

            split_x(0)
            split_x(1)
            dve.wait_ge(params_in, 16)
            dve.tensor_scalar(gain[:, :], par[:, EPS_AT:EPS_AT + 2], 1.0, 1.0, ALU.add, ALU.add).then_inc(gain_ready, 1)
            layer0_quarter(0, None)
            with dve.Fori(1, QUARTERS) as q:
                layer0_quarter(q, q - 1)
            layer1_quarter(0, None)
            with dve.Fori(1, QUARTERS) as q:
                layer1_quarter(q, q - 1)
            residual2(QUARTERS - 1)
            for k in range(0, KB, 2):
                statistics(2 * QUARTERS, k)
            statistics_taken(2 * QUARTERS)
            aggregate()

        @block.gpsimd
        def _(pool):
            def quarter(t, q):
                if isinstance(q, int):
                    return t[:, q, :].rearrange("p (k d) -> p k d", d=P)
                return t[:, bass.ds(q, 1), :].rearrange("p o (k d) -> p (o k) d", d=P)

            steps = [0]

            def bias_rows(at):
                return par[:, at:at + P].rearrange("p (o d) -> p o d", o=1).to_broadcast([P, KB, P])

            def residual0(q):
                wait(pool, z_ready, q)
                pool.tensor_tensor(xb[:, :, :], as_f32(quarter(x1hi, q)), as_f32(quarter(x1lo, q)),
                                   ALU.add).then_inc(xb_step, 1)
                wait(pool, xb_step, q + 1)
                pool.tensor_tensor(xb[:, :, :], xb[:, :, :], bias_rows(BM_AT), ALU.add).then_inc(xb_ready, 1)

            def norm_factors(done):
                wait(pool, stats_ready, done)
                pool.tensor_tensor(vareps[:, :], mv[:, :, 1], epsilons[:, :], ALU.add).then_inc(norm_step, 1)
                wait(pool, norm_step, (done - 1) * 3 + 1)
                pool.tensor_tensor(rstd[:, :], vareps[:, :], halves[:, :], ALU.pow).then_inc(norm_step, 1)
                wait(pool, norm_step, (done - 1) * 3 + 2)
                pool.tensor_tensor(shift[:, :], mv[:, :, 0], rstd[:, :], ALU.mult).then_inc(norm_step, 1)
                wait(pool, norm_step, (done - 1) * 3 + 3)
                pool.tensor_tensor(nshift[:, :], shift[:, :], minus[:, :], ALU.mult).then_inc(norm_ready, 1)

            def degree_factors(q):
                wait(pool, deg_ready, q * 2 + 2)
                pool.tensor_tensor(degpow[:, :], degc[:, :], halves[:, :], ALU.pow).then_inc(y_step, 1)
                wait(pool, y_step, q + 1)
                to = dall[:, q, :] if isinstance(q, int) else dall[:, bass.ds(q, 1), :].rearrange("p o k -> p (o k)")
                pool.tensor_tensor(to, degpow[:, :], degpos[:, :], ALU.mult).then_inc(y_step2, 1)

            def make_y(g):
                pool.wait_ge(block_used, (QUARTERS - 1) * JB + KB * (g + 1))
                pool.wait_ge(xn_ready, g + 1)
                pool.wait_ge(y_step2, g + 1)
                if g:
                    pool.wait_ge(y_ready, g)
                d = dall[:, g, :].rearrange("p (k o) -> p k o", o=1).to_broadcast([P, KB, P])
                pool.tensor_tensor(yt[:, :, :], quarter(xn, g), d, ALU.mult).then_inc(y_part, 1)
                pool.wait_ge(y_part, 2 * g + 1)
                pool.tensor_copy(quarter(x1hi, g), yt[:, :, :]).then_inc(y_part, 1)
                pool.wait_ge(y_part, 2 * g + 2)
                pool.tensor_tensor(quarter(x1lo, g), yt[:, :, :], as_f32(quarter(x1hi, g)),
                                   ALU.subtract).then_inc(y_ready, 1)

            def prepare_layer1(q):
                wait(pool, y_ready, q + 1) if isinstance(q, int) else None
                wait(pool, yd_added, q)
                flat = lambda t: (t[:, q, :] if isinstance(q, int)
                                  else t[:, bass.ds(q, 1), :].rearrange("p o f -> p (o f)"))
                pool.tensor_copy(ydhi[:, :], flat(x1hi)).then_inc(yd_ready, 1)
                pool.tensor_copy(ydlo[:, :], flat(x1lo)).then_inc(yd_ready, 1)
                wait(pool, z_ready, q + QUARTERS)
                dq = dall[:, q, :] if isinstance(q, int) else dall[:, bass.ds(q, 1), :].rearrange("p o k -> p (o k)")
                pool.tensor_copy(dcur[:, :], dq).then_inc(xb_step, 1)
                pool.tensor_tensor(xb[:, :, :], quarter(xn, q), bias_rows(BO_AT), ALU.add).then_inc(xb_ready, 1)

            pool.memset(ones[:, :], 1.0).then_inc(const_ready, 1)
            pool.memset(halves[:, :], -0.5).then_inc(const_ready, 1)
            pool.memset(epsilons[:, :], LN_EPS).then_inc(const_ready, 1)
            pool.memset(minus[:, :], -1.0).then_inc(const_ready, 1)
            pool.memset(ident[:, :], 0.0).then_inc(const_step, 1)
            pool.wait_ge(const_step, 1)
            pool.affine_select(out=ident[:, :], in_=ident[:, :], compare_op=ALU.not_equal, fill=1.0,
                               base=0, pattern=[[-1, P]], channel_multiplier=1).then_inc(const_step, 1)
            pool.wait_ge(const_step, 2)
            pool.tensor_copy(identr[:, :], ident[:, :]).then_inc(const_ready, 1)
            pool.wait_ge(const_ready, 5)
            pool.wait_ge(params_in, 16)
            pool.wait_ge(x_split, X_PIECES)
            with pool.Fori(0, QUARTERS - 1) as q:
                residual0(q)
                degree_factors(q)
                norm_factors(q + 1)
            residual0(QUARTERS - 1)
            for g in range(QUARTERS - 1):
                make_y(g)
            degree_factors(QUARTERS - 1)
            norm_factors(QUARTERS)
            make_y(QUARTERS - 1)
            pool.wait_ge(y_ready, QUARTERS)
            with pool.Fori(0, QUARTERS) as q:
                prepare_layer1(q)
                norm_factors(q + (QUARTERS + 1))


_OUT = (N, P)


def kernel(**inputs):
    import numpy as np
    import concourse.bacc as bacc
    from concourse.bass_utils import run_bass_kernel_spmd

    x = {k: np.asarray(v) for k, v in inputs.items()}
    a = x["adj"].reshape(QUARTERS, P, KB, QUARTERS, P, KB // 2, 2)
    a_t = np.ascontiguousarray(a.transpose(0, 3, 5, 4, 6, 2, 1)).reshape(QUARTERS * PAIRS, P, 2, QW)

    def layers(w):
        return w.transpose(2, 0, 1).reshape(P, LAYERS * P)

    rows = lambda v: np.broadcast_to(v.reshape(1, -1), (P, v.size))
    params = np.ascontiguousarray(np.concatenate([
        layers(x["L0_gnn_W1"]), layers(x["L0_gnn_W2"]),
        x["L0_gnn_Wm"].reshape(P, 2, P).transpose(2, 1, 0).reshape(P, 2 * P),
        x["L1_gnn_W"].T, rows(x["L0_gnn_bm"]), rows(x["L1_gnn_b"]),
        x["L0_gnn_b1"].T, x["L0_gnn_b2"].T, rows(x["L0_gnn_eps1"]), rows(x["L0_gnn_eps2"]),
    ], axis=1))
    arrays = {
        "a_t": a_t,
        "x1": np.ascontiguousarray(x["x"]).reshape(QUARTERS, P, QW),
        "x2": np.ascontiguousarray(x["L0_gnn_x2"]).reshape(QUARTERS, P, QW),
        "params": params,
    }
    nc = bacc.Bacc("TRN2", target_bir_lowering=False, num_devices=1)
    aps = [nc.dram_tensor(k, v.shape, F32, kind="ExternalInput").ap() for k, v in arrays.items()]
    out = nc.dram_tensor("out", (QUARTERS, P, QW), F32, kind="ExternalOutput").ap()
    build(nc, *aps, out)
    r = run_bass_kernel_spmd(nc, [arrays], core_ids=[0])
    return r.results[0]["out"].reshape(_OUT)
```

```python
from contextlib import ExitStack

import concourse.bass as bass
from concourse import mybir

F32 = mybir.dt.float32
F32R = mybir.dt.float32r
ALU = mybir.AluOpType
ACT = mybir.ActivationFunctionType

P = 128
N = 4096
QUARTERS = 4
QW = N // QUARTERS
KB = QW // P
HB = KB // 2
JB = N // P
PAIRS = JB // 2
CW = 512
CH = QW // CW
M = 2 * CH
LAYERS = 3
RAW = 4
RAW2 = 4
SPLIT = 4
LN_EPS = 1e-5
TINY = 1.1754944e-38

W1_AT = 0
W2_AT = W1_AT + LAYERS * P
WM_AT = W2_AT + LAYERS * P
WO_AT = WM_AT + 2 * P
BM_AT = WO_AT + P
BO_AT = BM_AT + P
B1_AT = BO_AT + P
B2_AT = B1_AT + LAYERS
EPS_AT = B2_AT + LAYERS
PARAMS = EPS_AT + 2

PE_DENSE = {3: 0, 5: 1, 8: 2}
PE_MERGE = 10
PE_PROJECT = 1
PE_ADD_Y = 28
ACT_EVACUATE = 2
ACT_RELU = {k + SPLIT: l for k, l in PE_DENSE.items()}
DVE_RESIDUAL = PE_MERGE + SPLIT
ACT_NORM = 22
ACT_COPY_Y = 10
DVE_RESIDUAL2 = PE_PROJECT + SPLIT
DVE_STATISTICS2 = DVE_RESIDUAL2 + KB
ACT_NORM2 = DVE_STATISTICS2 + KB + 4


X_PIECES = [(0, 0, 2), (0, 2, KB), (1, 0, KB), (2, 0, KB), (3, 0, KB)]
X_PIECE_AT = {KB * q + k: i for i, (q, k, _) in enumerate(X_PIECES)}
X_AFTER = {1: 1, 4: 2, 12: 3, 20: 4}
X_DVE = 2


def build(nc, a_t, x12, params, out):
    with ExitStack() as ctx:
        def sb(name, shape, dt=F32):
            return ctx.enter_context(nc.sbuf_tensor(name, shape, dt))

        def sem(name):
            return ctx.enter_context(nc.semaphore(name))

        x1hi = sb("x1hi", [P, QUARTERS, QW], F32R)
        x1lo = sb("x1lo", [P, QUARTERS, QW], F32R)
        with ExitStack() as first_use:
            x2s = first_use.enter_context(nc.sbuf_tensor("x2s", [P, QUARTERS, 2, QW], F32R))
            hlo = first_use.enter_context(nc.sbuf_tensor("hlo", [P, M, CW], F32R))
        raw2 = sb("raw2", [P, RAW2, 2, QW])
        yt = sb("yt", [P, KB, P])
        outn = sb("outn", [P, QW])
        x2hi, x2lo = x2s[:, :, 0, :], x2s[:, :, 1, :]
        xn = sb("xn", [P, QUARTERS, QW])
        raw = sb("raw", [P, RAW, 2, QW])
        ahi = sb("ahi", [P, SPLIT, QW], F32R)
        alo = sb("alo", [P, SPLIT, QW], F32R)
        h = sb("h", [P, M, CW])
        hhi = sb("hhi", [P, M, CW], F32R)
        rowsum = sb("rowsum", [P, QW])
        rowsum_all = sb("rowsum_all", [P, QW])
        xb = sb("xb", [P, KB, P])
        z = sb("z", [P, KB, P])
        ydhi, ydlo = (hhi[:, CH * i:CH * (i + 1), :].rearrange("p c w -> p (c w)") for i in range(2))
        par = sb("par", [P, PARAMS])
        whi = sb("whi", [P, WM_AT], F32R)
        wlo = sb("wlo", [P, WM_AT], F32R)
        gain = sb("gain", [P, 2])
        ones = sb("ones", [P, 1])
        ident = sb("ident", [P, P])
        identr = sb("identr", [P, P], F32R)
        halves = sb("halves", [P, KB])
        epsilons = sb("epsilons", [P, KB])
        minus = sb("minus", [P, KB])
        stats = sb("stats", [P, KB, 6])
        mv = sb("mv", [P, KB, 2])
        vareps = sb("vareps", [P, KB])
        rstd = sb("rstd", [P, KB])
        shift = sb("shift", [P, KB])
        nshift = sb("nshift", [P, KB])
        degc = sb("degc", [P, KB])
        degpos = sb("degpos", [P, KB])
        degpow = sb("degpow", [P, KB])
        dall = sb("dall", [P, QUARTERS, KB])
        dcur = sb("dcur", [P, KB])
        ps = [ctx.enter_context(nc.psum_tensor(f"ps{i}", [P, CW], F32)) for i in range(M)]
        pd = ctx.enter_context(nc.psum_tensor("pd", [P, M, CW], F32))
        merged = pd[:, 0:2, :].rearrange("p c (k d) -> p (c k) d", d=P)
        degree = pd[:, 2, 0:KB]

        params_in = sem("params_in")
        x_in = [sem(f"x_in{i}") for i in range(len(X_PIECES))]
        block0_in = sem("block0_in")
        raw_in = [sem(f"raw_in{i}") for i in range(RAW)]
        raw2_in = [sem(f"raw2_in{i}") for i in range(RAW2)]
        x_hi = sem("x_hi")
        x_split = sem("x_split")
        x_split2 = sem("x_split2")
        hi_ready = sem("hi_ready")
        lo_ready = sem("lo_ready")
        rowsum_step = sem("rowsum_step")
        raw_used = sem("raw_used")
        block_used = sem("block_used")
        ax_done = sem("ax_done")
        h_ready = sem("h_ready")
        hhi_ready = sem("hhi_ready")
        hlo_ready = sem("hlo_ready")
        dense_done = sem("dense_done")
        merge_done = sem("merge_done")
        xb_step = sem("xb_step")
        xb_ready = sem("xb_ready")
        deg_ready = sem("deg_ready")
        z_ready = sem("z_ready")
        stats_step = sem("stats_step")
        stats_ready = sem("stats_ready")
        norm_step = sem("norm_step")
        norm_ready = sem("norm_ready")
        xn_ready = sem("xn_ready")
        y_step = sem("y_step")
        y_step2 = sem("y_step2")
        y_part = sem("y_part")
        y_ready = sem("y_ready")
        yd_ready = sem("yd_ready")
        yd_added = sem("yd_added")
        ay_done = sem("ay_done")
        ay_copied = sem("ay_copied")
        project_done = sem("project_done")
        out_ready = sem("out_ready")
        out_written = sem("out_written")
        half_written = sem("half_written")
        const_step = sem("const_step")
        const_ready = sem("const_ready")
        gain_ready = sem("gain_ready")
        whi_ready = sem("whi_ready")
        wlo_ready = sem("wlo_ready")

        as_f32 = lambda ap: ap.bitcast(F32)

        def wait(eng, s, value):
            if not isinstance(value, int) or value > 0:
                eng.wait_ge(s, value)

        x_hi_parts = (x1hi, x2hi)
        x_lo_parts = (x1lo, x2lo)
        block_of = lambda t, j: t[:, j // KB, (j % KB) * P:(j % KB + 1) * P]

        def raw_tile(layer, n):
            p = n // 2
            if layer == 0:
                return raw[:, p % RAW, n % 2, :]
            p %= RAW + RAW2
            return raw[:, p, n % 2, :] if p < RAW else raw2[:, p - RAW, n % 2, :]

        block = ctx.enter_context(nc.Block())

        @block.sync
        def _(sp):
            def load_x(i):
                q, k0, k1 = X_PIECES[i]
                if q == 2:
                    sp.wait_ge(x_split, 2 * X_DVE)
                if q == 3:
                    sp.wait_ge(x_split2, 2)
                place = 2 * (q % 2)
                sp.dma_start(xn[:, place:place + 2, k0 * P:k1 * P],
                             x12[q][:, :, k0 * P:k1 * P]).then_inc(x_in[i], 16)

            load_x(0)
            sp.dma_start(raw[:, 0, 0], a_t[0][:, 0]).then_inc(block0_in, 16)
            sp.dma_start(raw[:, 0, 1], a_t[0][:, 1]).then_inc(raw_in[0], 16)
            load_x(1)
            for p in range(1, RAW):
                sp.dma_start(raw[:, p], a_t[p]).then_inc(raw_in[p], 16)
                if p == 1:
                    load_x(2)
            sp.dma_start(par[:, :], params).then_inc(params_in, 16)

            def load(dst, p):
                src = a_t[p] if isinstance(p, int) else a_t[bass.ds(p, 1)].rearrange("o p t i -> (o p) t i")
                return sp.dma_start(dst, src)

            def load0(g, s):
                sp.wait_ge(raw_used, g * RAW + (s + 1 - RAW))
                load(raw[:, s], g * RAW + s).then_inc(raw_in[s], 16)

            def load2(g):
                sp.wait_ge(block_used, (QUARTERS - 1) * JB + (g + 1) * KB)
                load(raw2[:, g], RAW + g).then_inc(raw2_in[g], 16)

            groups = QUARTERS * PAIRS // RAW
            for g in (1, 2):
                for s in range(RAW):
                    load0(g, s)
                load_x(2 + g)
            with sp.Fori(3, groups - 1) as g:
                for s in range(RAW):
                    load0(g, s)
            load2(0)
            for s in range(RAW):
                load0(groups - 1, s)
                if s == 1:
                    load2(1)
            for s in range(RAW):
                sp.wait_ge(raw_used, groups * RAW + s + 1 - RAW)
                load(raw[:, s], s).then_inc(raw_in[s], 16)
                if s == 0:
                    load2(2)
            load2(3)
            with sp.Fori(1, groups * RAW // (RAW + RAW2)) as g:
                for s in range(RAW + RAW2):
                    sp.wait_ge(lo_ready, g * (2 * (RAW + RAW2)) + (QUARTERS * JB + 2 * (s + 1 - RAW - RAW2)))
                    dst, landed = (raw[:, s], raw_in[s]) if s < RAW else (raw2[:, s - RAW], raw2_in[s - RAW])
                    load(dst, g * (RAW + RAW2) + s).then_inc(landed, 16)

        @block.tensor
        def _(pe):
            def products(q, layer, n, stationary, first_wait):
                at = q * JB + (layer * QUARTERS * JB + n + 1)
                banks = [(b, c) for b in range(len(stationary)) for c in range(CH)]
                hi = [ahi[:, n % SPLIT, c * CW:(c + 1) * CW] for c in range(CH)]
                lo = [alo[:, n % SPLIT, c * CW:(c + 1) * CW] for c in range(CH)]
                wait(pe, hi_ready, at)
                wait(pe, lo_ready, at)
                if n in (0, JB - 1):
                    order = [(b, c, k) for b, c in banks for k in range(3)]
                else:
                    order = [(b, c, k) for b in range(len(stationary)) for k in range(3) for c in range(CH)]
                for b, c, k in order:
                    whi, wlo = stationary[b]
                    w, a = ((whi, hi), (whi, lo), (wlo, hi))[k]
                    bank = b * CH + c
                    if n == 0 and k == 0:
                        first_wait(bank)
                    mm = pe.matmul(ps[bank][:, :], block_of(w, n), a[c],
                                   start=(n == 0 and k == 0), stop=(n == JB - 1 and k == 2))
                    if n == JB - 1 and k == 2 and (b, c) != banks[-1]:
                        mm.then_inc(ay_done if layer else ax_done, 1)
                mm.then_inc(block_used, 1)

            def dense(q, l):
                for m in range(M):
                    wait(pe, hlo_ready, q * (LAYERS * M) + (M * l + m + 1))
                    at = (W1_AT, W2_AT)[m // CH] + l * P
                    passes = ((whi, hhi), (whi, hlo), (wlo, hhi))
                    for k, (w, a) in enumerate(passes):
                        mm = pe.matmul(pd[:, m, :], w[:, at:at + P], a[:, m, :], start=(k == 0),
                                       stop=(k == len(passes) - 1))
                    mm.then_inc(dense_done, 1)

            def merge(q):
                wait(pe, h_ready, q * (4 * M) + 4 * M)
                for k in range(KB):
                    pe.matmul(degree[:, k:k + 1], rowsum_all[:, k * P:(k + 1) * P], ones[:, :],
                              start=(k == 0), stop=(k == KB - 1), skip_group_check=True)
                for k in range(KB):
                    for b in range(2):
                        mm = pe.matmul(merged[:, k, :], h[:, CH * b + k // 4, (k % 4) * P:(k % 4 + 1) * P],
                                       par[:, WM_AT + b * P:WM_AT + (b + 1) * P],
                                       start=(k % 4 == 0 and b == 0), stop=(k % 4 == 3 and b == 1),
                                       skip_group_check=True)
                mm.then_inc(merge_done, 1)

            def mlp_step(q, n):
                if n in PE_DENSE:
                    if n == min(PE_DENSE):
                        wait(pe, raw_used, q * PAIRS + PAIRS)
                        wait(pe, z_ready, q)
                        wait(pe, deg_ready, 2 * q)
                    dense(q, PE_DENSE[n])
                if n == PE_MERGE:
                    merge(q)

            def layer0_quarter(q, before):
                def empty(bank):
                    if before is not None:
                        wait(pe, h_ready, before * (4 * M) + (bank + 1))
                for n in range(JB):
                    if before is None and n in X_PIECE_AT:
                        i = X_PIECE_AT[n]
                        if i < X_DVE:
                            pe.wait_ge(x_split, 2 * (i + 1))
                        else:
                            pe.wait_ge(x_split2, 2 * (i + 1 - X_DVE))
                    products(q, 0, n, ((x1hi, x1lo), (x2hi, x2lo)), empty)
                    if before is not None:
                        mlp_step(before, n)

            def project(q, chunks=CH, blocks=range(KB)):
                wait(pe, ay_copied, q * CH + chunks)
                pe.wait_ge(z_ready, q + QUARTERS)
                for k in blocks:
                    mm = pe.matmul(merged[:, k, :], h[:, k // 4, (k % 4) * P:(k % 4 + 1) * P],
                                   par[:, WO_AT:WO_AT + P], start=(k % 4 == 0), stop=(k % 4 == 3),
                                   skip_group_check=True)
                mm.then_inc(project_done, 1)

            def layer1_quarter(q, before):
                def empty(bank):
                    if before is None:
                        wait(pe, h_ready, (QUARTERS - 1) * 4 * M + bank + 1)
                    else:
                        wait(pe, ay_copied, before * CH + (bank + 1))
                for n in range(JB):
                    if before is None and n % HB == 0:
                        pe.wait_ge(y_ready, n // HB + 1)
                    products(q, 1, n, ((x1hi, x1lo),), empty)
                    if n == PE_ADD_Y:
                        if before is None:
                            parts = (x1hi[:, 0, :], x1lo[:, 0, :])
                        else:
                            parts = (ydhi, ydlo)
                            wait(pe, yd_ready, q * 2)
                        for k in range(KB):
                            for part in parts:
                                mm = pe.matmul(ps[k // 4][:, (k % 4) * P:(k % 4 + 1) * P],
                                               part[:, k * P:(k + 1) * P], identr[:, :],
                                               start=False, stop=False)
                        mm.then_inc(yd_added, 1)
                    if before is None:
                        mlp_step(QUARTERS - 1, n)
                    elif n == PE_PROJECT:
                        project(before)

            pe.wait_ge(const_ready, 5)
            layer0_quarter(0, None)
            pe.wait_ge(params_in, 16)
            pe.wait_ge(wlo_ready, 1)
            with pe.Fori(1, QUARTERS) as q:
                layer0_quarter(q, q - 1)
            layer1_quarter(0, None)
            with pe.Fori(1, QUARTERS) as q:
                layer1_quarter(q, q - 1)
            for c in range(CH):
                project(QUARTERS - 1, c + 1, range(c * KB // CH, (c + 1) * KB // CH))

        @block.scalar
        def _(act):
            def round_x(i):
                q, k0, k1 = X_PIECES[i]
                act.wait_ge(x_in[i], 16)
                for b in range(2):
                    act.activation(x_hi_parts[b][:, q, k0 * P:k1 * P], xn[:, 2 * (q % 2) + b, k0 * P:k1 * P],
                                   ACT.Copy).then_inc(x_hi, 1)

            def round_a(q, layer, n):
                p = n // 2
                if layer == 0:
                    if n == 0 and isinstance(q, int) and q == 0:
                        act.wait_ge(block0_in, 16)
                    elif n % 2 == 0 or (n == 1 and isinstance(q, int) and q == 0):
                        act.wait_ge(raw_in[p % RAW], q * (16 * PAIRS // RAW) + 16 * (p // RAW + 1))
                elif n % 2 == 0:
                    s, turn = p % (RAW + RAW2), p // (RAW + RAW2)
                    per_quarter = 16 * PAIRS // (RAW + RAW2)
                    if s < RAW:
                        act.wait_ge(raw_in[s], q * per_quarter + 16 * (QUARTERS * PAIRS // RAW + turn + 1))
                    else:
                        act.wait_ge(raw2_in[s - RAW], q * per_quarter + 16 * (turn + 1))
                wait(act, block_used, q * JB + (layer * QUARTERS * JB + n + 1 - SPLIT))
                act.activation(ahi[:, n % SPLIT, :], raw_tile(layer, n), ACT.Copy).then_inc(hi_ready, 1)

            def round_h(q, l, m):
                wait(act, h_ready, q * (4 * M) + (M * l + m + 1))
                act.activation(hhi[:, m, :], h[:, m, :], ACT.Copy).then_inc(hhi_ready, 1)

            def evacuate(q):
                for m in range(M):
                    if m < M - 1:
                        wait(act, ax_done, q * (M - 1) + (m + 1))
                    else:
                        wait(act, block_used, q * JB + JB)
                    act.activation(h[:, m, :], ps[m][:, :], ACT.Identity,
                                   scale=gain[:, m // CH:m // CH + 1]).then_inc(h_ready, 1)

            def relu(q, l):
                for m in range(M):
                    wait(act, dense_done, q * (LAYERS * M) + (M * l + m + 1))
                    at = (B1_AT, B2_AT)[m // CH] + l
                    act.activation(h[:, m, :], pd[:, m, :], ACT.Relu,
                                   bias=par[:, at:at + 1]).then_inc(h_ready, 1)
                    if l < LAYERS - 1:
                        round_h(q, l + 1, m)

            def normalise(done, dst, ready, blocks):
                wait(act, norm_ready, done)
                for k in blocks:
                    i = act.activation(dst(k), z[:, k, :], ACT.Identity,
                                       scale=rstd[:, k:k + 1], bias=nshift[:, k:k + 1])
                    if k % HB == HB - 1:
                        i.then_inc(ready, 1)

            def mlp_step(q, n):
                if n == ACT_EVACUATE:
                    evacuate(q)
                if n in (ACT_EVACUATE + 1, ACT_EVACUATE + 2):
                    for m in range(CH):
                        round_h(q, 0, CH * (n - ACT_EVACUATE - 1) + m)
                if n in ACT_RELU:
                    relu(q, ACT_RELU[n])
                if ACT_NORM <= n < ACT_NORM + KB // 2:
                    if isinstance(q, int):
                        to = lambda k: xn[:, q, k * P:(k + 1) * P]
                    else:
                        to = lambda k: xn[:, bass.ds(q, 1), k * P:(k + 1) * P].rearrange("p o d -> p (o d)")
                    k = 2 * (n - ACT_NORM)
                    normalise(q + 1, to, xn_ready, (k, k + 1))

            def copy_ay(q):
                for c in range(CH):
                    if c < CH - 1:
                        wait(act, ay_done, q * (CH - 1) + (c + 1))
                    else:
                        wait(act, block_used, q * JB + (QUARTERS * JB + JB))
                    act.activation(h[:, c, :], ps[c][:, :], ACT.Copy).then_inc(ay_copied, 1)

            def copy_y(q, part):
                if part == 0:
                    wait(act, yd_added, q)
                act.activation((ydhi, ydlo)[part], (x1hi, x1lo)[part][:, bass.ds(q, 1), :].rearrange("p o f -> p (o f)"),
                               ACT.Copy).then_inc(yd_ready, 1)

            to_outn = lambda k: outn[:, k * P:(k + 1) * P]

            def finish(q, k):
                if k == 0:
                    wait(act, out_written, q * 16)
                normalise(q + (QUARTERS + 1), to_outn, out_ready, (k, k + 1))

            def store(q):
                wait(act, out_ready, q * 2 + 2)
                act.dma_start(out[bass.ds(q, 1)].rearrange("o p f -> (o p) f"), outn[:, :]).then_inc(out_written, 16)

            def layer0_quarter(q, before):
                for n in range(JB):
                    round_a(q, 0, n)
                    if before is not None:
                        mlp_step(before, n)
                    elif n in X_AFTER:
                        round_x(X_AFTER[n])

            def layer1_quarter(q, before):
                for n in range(JB):
                    round_a(q, 1, n)
                    if before is None:
                        mlp_step(QUARTERS - 1, n)
                    else:
                        if n == ACT_EVACUATE:
                            copy_ay(before)
                        if n in (ACT_COPY_Y, ACT_COPY_Y + 1):
                            copy_y(q, n - ACT_COPY_Y)
                        if ACT_NORM2 <= n < ACT_NORM2 + KB // 2:
                            finish(before, 2 * (n - ACT_NORM2))
                        if n == ACT_NORM2 + KB // 2:
                            store(before)

            round_x(0)
            layer0_quarter(0, None)
            act.wait_ge(params_in, 16)
            act.wait_ge(gain_ready, 1)
            act.activation(whi[:, :], par[:, 0:WM_AT], ACT.Copy).then_inc(whi_ready, 1)
            with act.Fori(1, QUARTERS) as q:
                layer0_quarter(q, q - 1)
            layer1_quarter(0, None)
            with act.Fori(1, QUARTERS) as q:
                layer1_quarter(q, q - 1)
            last = QUARTERS - 1
            copy_ay(last)
            act.wait_ge(out_written, 16 * last)
            normalise(QUARTERS + last + 1, to_outn, out_ready, range(0, HB))
            act.wait_ge(out_ready, 2 * last + 1)
            act.dma_start(out[last][:, 0:CW], outn[:, 0:CW]).then_inc(out_written, 16)
            act.wait_ge(out_ready, 2 * last + 2)
            act.dma_start(out[last][:, CW:QW], outn[:, CW:QW]).then_inc(half_written, 16)
            act.wait_ge(out_written, 16 * QUARTERS)
            act.wait_ge(half_written, 16)

        @block.vector
        def _(dve):
            def split_x(i):
                q, k0, k1 = X_PIECES[i]
                for b in range(2):
                    dve.wait_ge(x_hi, 2 * i + b + 1)
                    dve.tensor_tensor(x_lo_parts[b][:, q, k0 * P:k1 * P], xn[:, 2 * (q % 2) + b, k0 * P:k1 * P],
                                      as_f32(x_hi_parts[b][:, q, k0 * P:k1 * P]), ALU.subtract).then_inc(x_split, 1)

            def split_a(q, layer, n):
                wait(dve, hi_ready, q * JB + (layer * QUARTERS * JB + n + 1))
                dve.tensor_tensor(alo[:, n % SPLIT, :], raw_tile(layer, n),
                                  as_f32(ahi[:, n % SPLIT, :]), ALU.subtract).then_inc(lo_ready, 1)

            def sum_rows(q, n):
                tile = raw_tile(0, n)
                if n == 1:
                    wait(dve, raw_used, q * PAIRS)
                    dve.tensor_tensor(rowsum[:, :], raw[:, 0, 0, :], tile, ALU.add).then_inc(raw_used, 1)
                elif n % 2 == 0 and n:
                    wait(dve, raw_used, q * PAIRS + n // 2)
                    dve.tensor_tensor(rowsum[:, :], rowsum[:, :], tile, ALU.add).then_inc(rowsum_step, 1)
                elif n % 2:
                    wait(dve, rowsum_step, q * (PAIRS - 1) + n // 2)
                    to = rowsum_all if n == JB - 1 else rowsum
                    dve.tensor_tensor(to[:, :], rowsum[:, :], tile, ALU.add).then_inc(raw_used, 1)

            def degrees(q):
                dve.tensor_scalar(degc[:, :], degree, 1.0, TINY, ALU.add, ALU.max).then_inc(deg_ready, 1)
                dve.tensor_scalar(degpos[:, :], degree, 1.0, 0.0, ALU.add, ALU.is_gt).then_inc(deg_ready, 1)

            def statistics(done, blocks):
                if blocks[0] == 0:
                    wait(dve, z_ready, done)
                for i in blocks:
                    dve.bn_stats(stats[:, i, :], z[:, i, :]).then_inc(stats_step, 1)

            def statistics_taken(done):
                wait(dve, stats_step, done * KB)

            def aggregate(blocks=range(KB)):
                for k in blocks:
                    i = dve.bn_aggr(mv[:, k, :], stats[:, k, :])
                i.then_inc(stats_ready, 1)

            def residual(q):
                wait(dve, merge_done, q + 1)
                wait(dve, xb_ready, q + 1)
                wait(dve, xn_ready, q * 2)
                dve.tensor_tensor(z[:, :, :], merged, xb[:, :, :], ALU.add).then_inc(z_ready, 1)

            def mlp_step(q, n):
                if n == DVE_RESIDUAL:
                    residual(q)
                if n == DVE_RESIDUAL + 1:
                    degrees(q)
                if 0 <= n - DVE_RESIDUAL - 1 < KB // 2:
                    k = 2 * (n - DVE_RESIDUAL - 1)
                    statistics(q + 1, (k, k + 1))
                if n == DVE_RESIDUAL + KB // 2 + 1:
                    aggregate()

            def residual2(q, half, blocks, whole):
                if blocks[0] == half * HB:
                    wait(dve, project_done, q + (1 + half))
                    wait(dve, xb_ready, q + (QUARTERS + 1))
                    dve.wait_ge(xn_ready, 2 * QUARTERS)
                    wait(dve, out_ready, q * 2)
                for k in blocks:
                    i = dve.scalar_tensor_tensor(out=z[:, k, :], in0=merged[:, k, :], scalar=dcur[:, k:k + 1],
                                                 in1=xb[:, k, :], op0=ALU.mult, op1=ALU.add)
                    if k == whole:
                        i.then_inc(z_ready, 1)

            def finish_step(q, n):
                if 0 <= n - DVE_RESIDUAL2 < KB:
                    k = n - DVE_RESIDUAL2
                    residual2(q, 0, (k,), KB - 1)
                if 0 <= n - DVE_STATISTICS2 < KB:
                    statistics(q + (QUARTERS + 1), (n - DVE_STATISTICS2,))
                if n == DVE_STATISTICS2 + KB:
                    aggregate()

            def layer0_quarter(q, before):
                for n in range(JB):
                    if before is not None and n == DVE_RESIDUAL + KB // 2 + 1:
                        statistics_taken(before + 1)
                    split_a(q, 0, n)
                    sum_rows(q, n)
                    if before is not None:
                        mlp_step(before, n)
                    elif X_AFTER.get(n, X_DVE) < X_DVE:
                        split_x(X_AFTER[n])

            def layer1_quarter(q, before):
                for n in range(JB):
                    if before is None and n == DVE_RESIDUAL + KB // 2 + 1:
                        statistics_taken(QUARTERS)
                    elif before is not None and n == DVE_STATISTICS2 + KB:
                        statistics_taken(before + (QUARTERS + 1))
                    split_a(q, 1, n)
                    if before is None:
                        mlp_step(QUARTERS - 1, n)
                    else:
                        finish_step(before, n)

            split_x(0)
            layer0_quarter(0, None)
            dve.wait_ge(params_in, 16)
            dve.tensor_scalar(gain[:, :], par[:, EPS_AT:EPS_AT + 2], 1.0, 1.0, ALU.add, ALU.add).then_inc(gain_ready, 1)
            with dve.Fori(1, QUARTERS) as q:
                layer0_quarter(q, q - 1)
            layer1_quarter(0, None)
            with dve.Fori(1, QUARTERS) as q:
                layer1_quarter(q, q - 1)
            last = QUARTERS - 1
            for half in range(2):
                blocks = range(half * KB // 2, (half + 1) * KB // 2)
                residual2(last, half, blocks, blocks[-1])
                dve.wait_ge(z_ready, QUARTERS + last + 1 + half)
                for k in blocks:
                    dve.bn_stats(stats[:, k, :], z[:, k, :]).then_inc(stats_step, 1)
                dve.wait_ge(stats_step, (QUARTERS + last) * KB + (half + 1) * KB // 2)
                aggregate(blocks)
            dve.wait_ge(norm_ready, QUARTERS + last + 2)
            dve.wait_ge(out_ready, 2 * last + 1)
            for k in blocks:
                i = dve.tensor_scalar(outn[:, k * P:(k + 1) * P], z[:, k, :], rstd[:, k:k + 1], nshift[:, k:k + 1],
                                      ALU.mult, ALU.add)
            i.then_inc(out_ready, 1)

        @block.gpsimd
        def _(pool):
            def quarter(t, q):
                if isinstance(q, int):
                    return t[:, q, :].rearrange("p (k d) -> p k d", d=P)
                return t[:, bass.ds(q, 1), :].rearrange("p o (k d) -> p (o k) d", d=P)

            steps = [0]

            def bias_rows(at):
                return par[:, at:at + P].rearrange("p (o d) -> p o d", o=1).to_broadcast([P, KB, P])

            def split_h(q):
                for i in range(LAYERS * M):
                    wait(pool, hhi_ready, q * (LAYERS * M) + (i + 1))
                    m = i % M
                    pool.tensor_tensor(hlo[:, m, :], h[:, m, :], as_f32(hhi[:, m, :]),
                                       ALU.subtract).then_inc(hlo_ready, 1)

            def residual0(q):
                wait(pool, z_ready, q)
                pool.tensor_tensor(xb[:, :, :], as_f32(quarter(x1hi, q)), as_f32(quarter(x1lo, q)),
                                   ALU.add).then_inc(xb_step, 1)
                wait(pool, xb_step, q + 1)
                pool.tensor_tensor(xb[:, :, :], xb[:, :, :], bias_rows(BM_AT), ALU.add).then_inc(xb_ready, 1)

            def norm_factors(done, r=slice(0, KB)):
                wait(pool, stats_ready, done)
                pool.tensor_tensor(vareps[:, r], mv[:, r, 1], epsilons[:, r], ALU.add).then_inc(norm_step, 1)
                wait(pool, norm_step, (done - 1) * 3 + 1)
                pool.tensor_tensor(rstd[:, r], vareps[:, r], halves[:, r], ALU.pow).then_inc(norm_step, 1)
                wait(pool, norm_step, (done - 1) * 3 + 2)
                pool.tensor_tensor(shift[:, r], mv[:, r, 0], rstd[:, r], ALU.mult).then_inc(norm_step, 1)
                wait(pool, norm_step, (done - 1) * 3 + 3)
                pool.tensor_tensor(nshift[:, r], shift[:, r], minus[:, r], ALU.mult).then_inc(norm_ready, 1)

            def degree_factors(q):
                wait(pool, deg_ready, q * 2 + 2)
                pool.tensor_tensor(degpow[:, :], degc[:, :], halves[:, :], ALU.pow).then_inc(y_step, 1)
                wait(pool, y_step, q + 1)
                to = dall[:, q, :] if isinstance(q, int) else dall[:, bass.ds(q, 1), :].rearrange("p o k -> p (o k)")
                pool.tensor_tensor(to, degpow[:, :], degpos[:, :], ALU.mult).then_inc(y_step2, 1)

            def make_y(g, half):
                done = 2 * g + half
                r = slice(half * HB, (half + 1) * HB)
                pool.wait_ge(block_used, (QUARTERS - 1) * JB + KB * (g + 1))
                pool.wait_ge(xn_ready, done + 1)
                pool.wait_ge(y_step2, g + 1)
                if done:
                    pool.wait_ge(y_ready, done)
                d = dall[:, g, r].rearrange("p (k o) -> p k o", o=1).to_broadcast([P, HB, P])
                hi, lo = quarter(x1hi, g)[:, r, :], quarter(x1lo, g)[:, r, :]
                pool.tensor_tensor(yt[:, r, :], quarter(xn, g)[:, r, :], d, ALU.mult).then_inc(y_part, 1)
                pool.wait_ge(y_part, 2 * done + 1)
                pool.tensor_copy(hi, yt[:, r, :]).then_inc(y_part, 1)
                pool.wait_ge(y_part, 2 * done + 2)
                pool.tensor_tensor(lo, yt[:, r, :], as_f32(hi), ALU.subtract).then_inc(y_ready, 1)

            def prepare_layer1(q):
                wait(pool, z_ready, q + QUARTERS)
                dq = dall[:, q, :] if isinstance(q, int) else dall[:, bass.ds(q, 1), :].rearrange("p o k -> p (o k)")
                pool.tensor_copy(dcur[:, :], dq).then_inc(xb_step, 1)
                pool.tensor_tensor(xb[:, :, :], quarter(xn, q), bias_rows(BO_AT), ALU.add).then_inc(xb_ready, 1)

            pool.memset(ones[:, :], 1.0).then_inc(const_ready, 1)
            pool.memset(halves[:, :], -0.5).then_inc(const_ready, 1)
            pool.memset(epsilons[:, :], LN_EPS).then_inc(const_ready, 1)
            pool.memset(minus[:, :], -1.0).then_inc(const_ready, 1)
            pool.memset(ident[:, :], 0.0).then_inc(const_step, 1)
            pool.wait_ge(const_step, 1)
            pool.affine_select(out=ident[:, :], in_=ident[:, :], compare_op=ALU.not_equal, fill=1.0,
                               base=0, pattern=[[-1, P]], channel_multiplier=1).then_inc(const_step, 1)
            pool.wait_ge(const_step, 2)
            pool.tensor_copy(identr[:, :], ident[:, :]).then_inc(const_ready, 1)
            for i in range(X_DVE, len(X_PIECES)):
                q = X_PIECES[i][0]
                for b in range(2):
                    pool.wait_ge(x_hi, 2 * i + b + 1)
                    pool.tensor_tensor(x_lo_parts[b][:, q, :], xn[:, 2 * (q % 2) + b, :],
                                       as_f32(x_hi_parts[b][:, q, :]), ALU.subtract).then_inc(x_split2, 1)
            pool.wait_ge(const_ready, 5)
            pool.wait_ge(params_in, 16)
            pool.wait_ge(x_split, 2 * X_DVE)
            pool.wait_ge(x_split2, 2 * (len(X_PIECES) - X_DVE))
            pool.wait_ge(whi_ready, 1)
            pool.tensor_tensor(wlo[:, :], par[:, 0:WM_AT], as_f32(whi[:, :]), ALU.subtract).then_inc(wlo_ready, 1)
            with pool.Fori(0, QUARTERS - 1) as q:
                residual0(q)
                split_h(q)
                degree_factors(q)
                norm_factors(q + 1)
            residual0(QUARTERS - 1)
            for g in range(QUARTERS - 1):
                make_y(g, 0)
                make_y(g, 1)
            pool.wait_ge(y_ready, 2 * (QUARTERS - 1))
            split_h(QUARTERS - 1)
            degree_factors(QUARTERS - 1)
            norm_factors(QUARTERS)
            make_y(QUARTERS - 1, 0)
            make_y(QUARTERS - 1, 1)
            pool.wait_ge(y_ready, 2 * QUARTERS)
            with pool.Fori(0, QUARTERS - 1) as q:
                prepare_layer1(q)
                norm_factors(q + (QUARTERS + 1))
            prepare_layer1(QUARTERS - 1)
            for half in range(2):
                norm_factors(2 * QUARTERS + half, slice(half * KB // 2, (half + 1) * KB // 2))


_OUT = (N, P)


def kernel(**inputs):
    import numpy as np
    import concourse.bacc as bacc
    from concourse.bass_utils import run_bass_kernel_spmd

    x = {k: np.asarray(v) for k, v in inputs.items()}
    a = x["adj"].reshape(QUARTERS, P, KB, QUARTERS, P, KB // 2, 2)
    a_t = np.ascontiguousarray(a.transpose(0, 3, 5, 4, 6, 2, 1)).reshape(QUARTERS * PAIRS, P, 2, QW)

    def layers(w):
        return w.transpose(2, 0, 1).reshape(P, LAYERS * P)

    rows = lambda v: np.broadcast_to(v.reshape(1, -1), (P, v.size))
    params = np.ascontiguousarray(np.concatenate([
        layers(x["L0_gnn_W1"]), layers(x["L0_gnn_W2"]),
        x["L0_gnn_Wm"].reshape(P, 2, P).transpose(2, 1, 0).reshape(P, 2 * P),
        x["L1_gnn_W"].T, rows(x["L0_gnn_bm"]), rows(x["L1_gnn_b"]),
        x["L0_gnn_b1"].T, x["L0_gnn_b2"].T, rows(x["L0_gnn_eps1"]), rows(x["L0_gnn_eps2"]),
    ], axis=1))
    arrays = {
        "a_t": a_t,
        "x12": np.ascontiguousarray(np.stack([x["x"].reshape(QUARTERS, P, QW),
                                              x["L0_gnn_x2"].reshape(QUARTERS, P, QW)], axis=2)),
        "params": params,
    }
    nc = bacc.Bacc("TRN2", target_bir_lowering=False, num_devices=1)
    aps = [nc.dram_tensor(k, v.shape, F32, kind="ExternalInput").ap() for k, v in arrays.items()]
    out = nc.dram_tensor("out", (QUARTERS, P, QW), F32, kind="ExternalOutput").ap()
    build(nc, *aps, out)
    r = run_bass_kernel_spmd(nc, [arrays], core_ids=[0])
    return r.results[0]["out"].reshape(_OUT)
```

```python
from contextlib import ExitStack

import concourse.bass as bass
from concourse import mybir

F32 = mybir.dt.float32
F32R = mybir.dt.float32r
ALU = mybir.AluOpType
ACT = mybir.ActivationFunctionType

P = 128
N = 4096
QUARTERS = 4
QW = N // QUARTERS
KB = QW // P
HB = KB // 2
JB = N // P
PAIRS = JB // 2
CW = 512
CH = QW // CW
M = 2 * CH
LAYERS = 3
RAW = 4
RAW2 = 4
SPLIT = 4
LN_EPS = 1e-5
TINY = 1.1754944e-38

W1_AT = 0
W2_AT = W1_AT + LAYERS * P
WM_AT = W2_AT + LAYERS * P
WO_AT = WM_AT + 2 * P
BM_AT = WO_AT + P
BO_AT = BM_AT + P
B1_AT = BO_AT + P
B2_AT = B1_AT + LAYERS
EPS_AT = B2_AT + LAYERS
PARAMS = EPS_AT + 2

PE_DENSE = ({3: 0, 5: 1, 8: 2}, {1: 0, 3: 1, 5: 2})
PE_MERGE = (10, 7)
PE_PROJECT = 1
ACT_EVACUATE = 2
ACT_RELU = tuple({k + SPLIT: l for k, l in plan.items()} for plan in PE_DENSE)
DVE_RESIDUAL = tuple(k + SPLIT for k in PE_MERGE)
STATISTICS = (2, 4)
DVE_AGGREGATE = tuple(k + 1 + KB // s for k, s in zip(DVE_RESIDUAL, STATISTICS))
ACT_NORM = (22, 18)
ACT_COPY_AY = 1
ACT_ROUND_Y = (23, 26)
DVE_RESIDUAL2 = PE_PROJECT + SPLIT
DVE_STATISTICS2 = DVE_RESIDUAL2 + KB
DVE_AGGREGATE2 = DVE_STATISTICS2 + KB // 2
ACT_NORM2 = DVE_AGGREGATE2 + 6
POOL_NORM2 = 24


X_PIECES = [(0, 0, 2), (0, 2, 4), (0, 4, KB), (1, 0, KB), (2, 0, KB), (3, 0, KB)]
X_PIECE_AT = {KB * q + k: i for i, (q, k, _) in enumerate(X_PIECES)}
X_AFTER = {1: 1, 3: 2, 7: 3, 12: 4, 20: 5}
X_DVE = 3


def build(nc, a_t, x12, params, out):
    with ExitStack() as ctx:
        def sb(name, shape, dt=F32):
            return ctx.enter_context(nc.sbuf_tensor(name, shape, dt))

        def sem(name):
            return ctx.enter_context(nc.semaphore(name))

        x1hi = sb("x1hi", [P, QUARTERS, QW], F32R)
        x1lo = sb("x1lo", [P, QUARTERS, QW], F32R)
        with ExitStack() as first_use:
            x2s = first_use.enter_context(nc.sbuf_tensor("x2s", [P, QUARTERS, 2, QW], F32R))
            hlo = first_use.enter_context(nc.sbuf_tensor("hlo", [P, M, CW], F32R))
        raw2 = sb("raw2", [P, RAW2, 2, QW])
        yt = sb("yt", [P, KB, P])
        outn = sb("outn", [P, QW])
        x2hi, x2lo = x2s[:, :, 0, :], x2s[:, :, 1, :]
        xn = sb("xn", [P, QUARTERS, QW])
        raw = sb("raw", [P, RAW, 2, QW])
        ahi = sb("ahi", [P, SPLIT, QW], F32R)
        alo = sb("alo", [P, SPLIT, QW], F32R)
        h = sb("h", [P, M, CW])
        hhi = sb("hhi", [P, M, CW], F32R)
        rowsum = sb("rowsum", [P, QW])
        rowsum_all = sb("rowsum_all", [P, QW])
        xb = sb("xb", [P, KB, P])
        z = sb("z", [P, KB, P])
        par = sb("par", [P, PARAMS])
        whi = sb("whi", [P, WM_AT], F32R)
        wlo = sb("wlo", [P, WM_AT], F32R)
        gain = sb("gain", [P, 2])
        ones = sb("ones", [P, 1])
        identity = sb("identity", [P, P])
        halves = sb("halves", [P, KB])
        epsilons = sb("epsilons", [P, KB])
        minus = sb("minus", [P, KB])
        stats = sb("stats", [P, KB, 6])
        mv = sb("mv", [P, KB, 2])
        vareps = sb("vareps", [P, KB])
        rstd = sb("rstd", [P, KB])
        shift = sb("shift", [P, KB])
        nshift = sb("nshift", [P, KB])
        degc = sb("degc", [P, KB])
        degpos = sb("degpos", [P, KB])
        degpow = sb("degpow", [P, KB])
        dall = sb("dall", [P, QUARTERS, KB])
        dcur = sb("dcur", [P, KB])
        ps = [ctx.enter_context(nc.psum_tensor(f"ps{i}", [P, CW], F32)) for i in range(M)]
        pd = ctx.enter_context(nc.psum_tensor("pd", [P, M, CW], F32))
        merged = pd[:, 0:2, :].rearrange("p c (k d) -> p (c k) d", d=P)
        degree = pd[:, 2, 0:KB]

        params_in = sem("params_in")
        x_in = [sem(f"x_in{i}") for i in range(len(X_PIECES))]
        half_in = [sem(f"half_in{c}") for c in range(CH)]
        even_in = [None] + [sem(f"even_in{p}") for p in range(1, RAW)]
        raw_in = [sem(f"raw_in{i}") for i in range(RAW)]
        raw2_in = [sem(f"raw2_in{i}") for i in range(RAW2)]
        x_hi = sem("x_hi")
        x_split = sem("x_split")
        x_split2 = sem("x_split2")
        hi_ready = sem("hi_ready")
        lo_ready = sem("lo_ready")
        hi_half = sem("hi_half")
        lo_half = sem("lo_half")
        rowsum_step = sem("rowsum_step")
        raw_used = sem("raw_used")
        block_used = sem("block_used")
        ax_done = sem("ax_done")
        h_ready = sem("h_ready")
        hhi_ready = sem("hhi_ready")
        hlo_ready = sem("hlo_ready")
        dense_done = sem("dense_done")
        merge_done = sem("merge_done")
        xb_step = sem("xb_step")
        xb_ready = sem("xb_ready")
        deg_ready = sem("deg_ready")
        z_ready = sem("z_ready")
        stats_step = sem("stats_step")
        stats_ready = sem("stats_ready")
        norm_step = sem("norm_step")
        norm_ready = sem("norm_ready")
        xn_ready = sem("xn_ready")
        y_step = sem("y_step")
        y_step2 = sem("y_step2")
        yt_ready = sem("yt_ready")
        y_part = sem("y_part")
        yhi_ready = sem("yhi_ready")
        y_ready = sem("y_ready")
        identity_added = sem("identity_added")
        ay_done = sem("ay_done")
        ay_copied = sem("ay_copied")
        project_done = sem("project_done")
        out_ready = sem("out_ready")
        out_written = sem("out_written")
        half_written = sem("half_written")
        const_step = sem("const_step")
        const_ready = sem("const_ready")
        gain_ready = sem("gain_ready")
        whi_ready = sem("whi_ready")
        wlo_ready = sem("wlo_ready")

        as_f32 = lambda ap: ap.bitcast(F32)

        def wait(eng, s, value):
            if not isinstance(value, int) or value > 0:
                eng.wait_ge(s, value)

        x_hi_parts = (x1hi, x2hi)
        x_lo_parts = (x1lo, x2lo)
        block_of = lambda t, j: t[:, j // KB, (j % KB) * P:(j % KB + 1) * P]

        def raw_tile(layer, n):
            p = n // 2
            if layer == 0:
                return raw[:, p % RAW, n % 2, :]
            p %= RAW + RAW2
            return raw[:, p, n % 2, :] if p < RAW else raw2[:, p - RAW, n % 2, :]

        def wait_raw1(eng, q, n):
            s, turn = n // 2 % (RAW + RAW2), n // 2 // (RAW + RAW2)
            per_quarter = 16 * PAIRS // (RAW + RAW2)
            if s < RAW:
                eng.wait_ge(raw_in[s], q * per_quarter + 16 * (QUARTERS * PAIRS // RAW + turn + 1))
            else:
                eng.wait_ge(raw2_in[s - RAW], q * per_quarter + 16 * (turn + 1))

        def identities(q, n):
            if isinstance(q, int):
                return q * KB + min(max(n - q * KB + 1, 0), KB)
            assert QUARTERS == 4
            step = identities(2, n) - identities(1, n)
            return q * step + (identities(1, n) - step) if step else identities(1, n)

        def on_diagonal(q, n):
            return n // KB == q if isinstance(q, int) else KB <= n < 3 * KB

        block = ctx.enter_context(nc.Block())

        @block.sync
        def _(sp):
            def load_x(i):
                q, k0, k1 = X_PIECES[i]
                if q == 2:
                    sp.wait_ge(x_split, 2 * X_DVE)
                if q == 3:
                    sp.wait_ge(x_split2, 2)
                place = 2 * (q % 2)
                sp.dma_start(xn[:, place:place + 2, k0 * P:k1 * P],
                             x12[q][:, :, k0 * P:k1 * P]).then_inc(x_in[i], 16)

            load_x(0)
            for c in range(CH):
                cols = slice(c * CW, (c + 1) * CW)
                sp.dma_start(raw[:, 0, 0, cols], a_t[0][:, 0, cols]).then_inc(half_in[c], 16)
            sp.dma_start(raw[:, 0, 1], a_t[0][:, 1]).then_inc(raw_in[0], 16)
            load_x(1)
            for p in range(1, RAW):
                sp.dma_start(raw[:, p, 0], a_t[p][:, 0]).then_inc(even_in[p], 16)
                sp.dma_start(raw[:, p, 1], a_t[p][:, 1]).then_inc(raw_in[p], 16)
                if p in (1, 3):
                    load_x(2 + p // 2)
            sp.dma_start(par[:, :], params).then_inc(params_in, 16)

            def load(dst, p):
                src = a_t[p] if isinstance(p, int) else a_t[bass.ds(p, 1)].rearrange("o p t i -> (o p) t i")
                return sp.dma_start(dst, src)

            def load0(g, s):
                sp.wait_ge(raw_used, g * RAW + (s + 1 - RAW))
                load(raw[:, s], g * RAW + s).then_inc(raw_in[s], 16)

            def load2(g):
                sp.wait_ge(block_used, (QUARTERS - 1) * JB + (g + 1) * KB)
                load(raw2[:, g], RAW + g).then_inc(raw2_in[g], 16)

            groups = QUARTERS * PAIRS // RAW
            for g in (1, 2):
                for s in range(RAW):
                    load0(g, s)
                load_x(3 + g)
            with sp.Fori(3, groups - 1) as g:
                for s in range(RAW):
                    load0(g, s)
            load2(0)
            for s in range(RAW):
                load0(groups - 1, s)
                if s == 1:
                    load2(1)
            for s in range(RAW):
                sp.wait_ge(raw_used, groups * RAW + s + 1 - RAW)
                load(raw[:, s], s).then_inc(raw_in[s], 16)
                if s == 0:
                    load2(2)
            load2(3)
            with sp.Fori(1, groups * RAW // (RAW + RAW2)) as g:
                for s in range(RAW + RAW2):
                    sp.wait_ge(lo_ready, g * (2 * (RAW + RAW2)) + (QUARTERS * JB + 2 * (s + 1 - RAW - RAW2)))
                    dst, landed = (raw[:, s], raw_in[s]) if s < RAW else (raw2[:, s - RAW], raw2_in[s - RAW])
                    load(dst, g * (RAW + RAW2) + s).then_inc(landed, 16)

        @block.tensor
        def _(pe):
            def products(q, layer, n, stationary, first_wait):
                at = q * JB + (layer * QUARTERS * JB + n + 1)
                banks = [(b, c) for b in range(len(stationary)) for c in range(CH)]
                hi = [ahi[:, n % SPLIT, c * CW:(c + 1) * CW] for c in range(CH)]
                lo = [alo[:, n % SPLIT, c * CW:(c + 1) * CW] for c in range(CH)]
                first = isinstance(at, int) and at == 1
                if not first:
                    wait(pe, hi_ready, at)
                    wait(pe, lo_ready, at)
                if n in (0, JB - 1):
                    order = [(b, c, k) for b, c in banks for k in range(3)]
                else:
                    order = [(b, c, k) for b in range(len(stationary)) for k in range(3) for c in range(CH)]
                for b, c, k in order:
                    whi, wlo = stationary[b]
                    w, a = ((whi, hi), (whi, lo), (wlo, hi))[k]
                    bank = b * CH + c
                    if n == 0 and k == 0:
                        first_wait(bank)
                        if first and b == 0:
                            pe.wait_ge(lo_half if c == 0 else lo_ready, 1)
                    mm = pe.matmul(ps[bank][:, :], block_of(w, n), a[c],
                                   start=(n == 0 and k == 0), stop=(n == JB - 1 and k == 2))
                    if n == JB - 1 and k == 2 and (b, c) != banks[-1]:
                        mm.then_inc(ay_done if layer else ax_done, 1)
                mm.then_inc(block_used, 1)

            def dense(q, l, plan):
                for m in range(M):
                    if plan == 0:
                        wait(pe, hlo_ready, q * (LAYERS * M) + (M * l + m + 1))
                        passes = ((whi, hhi), (whi, hlo), (wlo, hhi))
                    else:
                        wait(pe, h_ready, q * (4 * M) + (M * l + m + 1))
                        passes = ((par, h),)
                    at = (W1_AT, W2_AT)[m // CH] + l * P
                    for k, (w, a) in enumerate(passes):
                        mm = pe.matmul(pd[:, m, :], w[:, at:at + P], a[:, m, :], start=(k == 0),
                                       stop=(k == len(passes) - 1))
                    mm.then_inc(dense_done, 1)

            def merge(q):
                wait(pe, h_ready, q * (4 * M) + 4 * M)
                for k in range(KB):
                    pe.matmul(degree[:, k:k + 1], rowsum_all[:, k * P:(k + 1) * P], ones[:, :],
                              start=(k == 0), stop=(k == KB - 1), skip_group_check=True)
                for k in range(KB):
                    for b in range(2):
                        mm = pe.matmul(merged[:, k, :], h[:, CH * b + k // 4, (k % 4) * P:(k % 4 + 1) * P],
                                       par[:, WM_AT + b * P:WM_AT + (b + 1) * P],
                                       start=(k % 4 == 0 and b == 0), stop=(k % 4 == 3 and b == 1),
                                       skip_group_check=True)
                mm.then_inc(merge_done, 1)

            def mlp_step(q, n, plan):
                if n in PE_DENSE[plan]:
                    if n == min(PE_DENSE[plan]):
                        wait(pe, raw_used, q * PAIRS + PAIRS)
                        wait(pe, z_ready, q)
                        wait(pe, deg_ready, 2 * q)
                    dense(q, PE_DENSE[plan][n], plan)
                if n == PE_MERGE[plan]:
                    merge(q)

            def layer0_quarter(q, before):
                def empty(bank):
                    if before is not None:
                        wait(pe, h_ready, before * (4 * M) + (bank + 1))
                for n in range(JB):
                    if before is None and n in X_PIECE_AT:
                        i = X_PIECE_AT[n]
                        if i < X_DVE:
                            pe.wait_ge(x_split, 2 * (i + 1))
                        else:
                            pe.wait_ge(x_split2, 2 * (i + 1 - X_DVE))
                    products(q, 0, n, ((x1hi, x1lo), (x2hi, x2lo)), empty)
                    if before is not None:
                        mlp_step(before, n, 0)

            def project(q, chunks=CH, blocks=range(KB)):
                wait(pe, ay_copied, q * CH + chunks)
                pe.wait_ge(z_ready, q + QUARTERS)
                for k in blocks:
                    mm = pe.matmul(merged[:, k, :], h[:, k // 4, (k % 4) * P:(k % 4 + 1) * P],
                                   par[:, WO_AT:WO_AT + P], start=(k % 4 == 0), stop=(k % 4 == 3),
                                   skip_group_check=True)
                mm.then_inc(project_done, 1)

            def last_products(q):
                for c in range(CH):
                    for n in range(JB - SPLIT, JB):
                        if c == 0:
                            pe.wait_ge(hi_ready, (QUARTERS + q) * JB + n + 1)
                            pe.wait_ge(lo_ready, (QUARTERS + q) * JB + n + 1)
                        for k, (w, a) in enumerate(((x1hi, ahi), (x1hi, alo), (x1lo, ahi))):
                            mm = pe.matmul(ps[c][:, :], block_of(w, n), a[:, n % SPLIT, c * CW:(c + 1) * CW],
                                           start=False, stop=(n == JB - 1 and k == 2))
                        if c == CH - 1:
                            mm.then_inc(block_used, 1)
                            if n == JB - SPLIT + 1:
                                project(q, 1, range(KB // CH))
                    if c < CH - 1:
                        mm.then_inc(ay_done, 1)

            def layer1_quarter(q, before):
                def empty(bank):
                    if before is None:
                        wait(pe, h_ready, (QUARTERS - 1) * 4 * M + bank + 1)
                    else:
                        wait(pe, ay_copied, before * CH + (bank + 1))
                last = isinstance(q, int) and q == QUARTERS - 1
                for n in range(JB - SPLIT if last else JB):
                    if before is None and n % HB == 0:
                        pe.wait_ge(y_ready, n // HB + 1)
                    products(q, 1, n, ((x1hi, x1lo),), empty)
                    if before is None:
                        mlp_step(QUARTERS - 1, n, 1)
                    elif n == PE_PROJECT:
                        project(before)
                if last:
                    last_products(q)

            pe.wait_ge(const_ready, 5)
            layer0_quarter(0, None)
            pe.wait_ge(params_in, 16)
            pe.wait_ge(wlo_ready, 1)
            with pe.Fori(1, QUARTERS) as q:
                layer0_quarter(q, q - 1)
            layer1_quarter(0, None)
            with pe.Fori(1, QUARTERS - 1) as q:
                layer1_quarter(q, q - 1)
            layer1_quarter(QUARTERS - 1, QUARTERS - 2)
            project(QUARTERS - 1, CH, range(KB // CH, KB))

        @block.scalar
        def _(act):
            def round_x(i):
                q, k0, k1 = X_PIECES[i]
                act.wait_ge(x_in[i], 16)
                for b in range(2):
                    act.activation(x_hi_parts[b][:, q, k0 * P:k1 * P], xn[:, 2 * (q % 2) + b, k0 * P:k1 * P],
                                   ACT.Copy).then_inc(x_hi, 1)

            def round_a(q, layer, n):
                p = n // 2
                if layer == 0:
                    start = isinstance(q, int) and q == 0 and p < RAW
                    if start and n == 0:
                        for c in range(CH):
                            act.wait_ge(half_in[c], 16)
                            act.activation(ahi[:, 0, c * CW:(c + 1) * CW], raw[:, 0, 0, c * CW:(c + 1) * CW],
                                           ACT.Copy).then_inc((hi_half, hi_ready)[c], 1)
                        return
                    if start and n % 2 == 0:
                        act.wait_ge(even_in[p], 16)
                    elif n % 2 == 0 or start:
                        act.wait_ge(raw_in[p % RAW], q * (16 * PAIRS // RAW) + 16 * (p // RAW + 1))
                else:
                    if n % 2 == 0:
                        wait_raw1(act, q, n)
                    if on_diagonal(q, n):
                        act.wait_ge(identity_added, identities(q, n))
                wait(act, block_used, q * JB + (layer * QUARTERS * JB + n + 1 - SPLIT))
                act.activation(ahi[:, n % SPLIT, :], raw_tile(layer, n), ACT.Copy).then_inc(hi_ready, 1)

            def round_h(q, l, m):
                wait(act, h_ready, q * (4 * M) + (M * l + m + 1))
                act.activation(hhi[:, m, :], h[:, m, :], ACT.Copy).then_inc(hhi_ready, 1)

            def evacuate(q):
                for m in range(M):
                    if m < M - 1:
                        wait(act, ax_done, q * (M - 1) + (m + 1))
                    else:
                        wait(act, block_used, q * JB + JB)
                    act.activation(h[:, m, :], ps[m][:, :], ACT.Identity,
                                   scale=gain[:, m // CH:m // CH + 1]).then_inc(h_ready, 1)

            def relu(q, l, plan):
                for m in range(M):
                    wait(act, dense_done, q * (LAYERS * M) + (M * l + m + 1))
                    at = (B1_AT, B2_AT)[m // CH] + l
                    act.activation(h[:, m, :], pd[:, m, :], ACT.Relu,
                                   bias=par[:, at:at + 1]).then_inc(h_ready, 1)
                    if plan == 0 and l < LAYERS - 1:
                        round_h(q, l + 1, m)

            def normalise(done, dst, ready, blocks):
                wait(act, norm_ready, done)
                for k in blocks:
                    i = act.activation(dst(k), z[:, k, :], ACT.Identity,
                                       scale=rstd[:, k:k + 1], bias=nshift[:, k:k + 1])
                    if k % HB == HB - 1:
                        i.then_inc(ready, 1)

            def mlp_step(q, n, plan):
                if n == ACT_EVACUATE:
                    evacuate(q)
                if plan == 0 and n in (ACT_EVACUATE + 1, ACT_EVACUATE + 2):
                    for m in range(CH):
                        round_h(q, 0, CH * (n - ACT_EVACUATE - 1) + m)
                if n in ACT_RELU[plan]:
                    relu(q, ACT_RELU[plan][n], plan)
                at, size = ACT_NORM[plan], 2
                if at <= n < at + KB // size:
                    if isinstance(q, int):
                        to = lambda k: xn[:, q, k * P:(k + 1) * P]
                    else:
                        to = lambda k: xn[:, bass.ds(q, 1), k * P:(k + 1) * P].rearrange("p o d -> p (o d)")
                    normalise(q + 1, to, xn_ready, range(size * (n - at), size * (n - at + 1)))
                if plan == 1 and n in ACT_ROUND_Y:
                    half = ACT_ROUND_Y.index(n)
                    act.wait_ge(yt_ready, 2 * q + half + 1)
                    act.activation(x1hi[:, q, half * CW:(half + 1) * CW],
                                   yt[:, half * HB:(half + 1) * HB, :].rearrange("p k d -> p (k d)"),
                                   ACT.Copy).then_inc(yhi_ready, 1)

            def copy_ay(q):
                for c in range(CH):
                    if c < CH - 1:
                        wait(act, ay_done, q * (CH - 1) + (c + 1))
                    else:
                        wait(act, block_used, q * JB + (QUARTERS * JB + JB))
                    act.activation(h[:, c, :], ps[c][:, :], ACT.Copy).then_inc(ay_copied, 1)

            to_outn = lambda k: outn[:, k * P:(k + 1) * P]

            def finish(q, k):
                if k == 0:
                    wait(act, out_written, q * 16)
                normalise(q + (QUARTERS + 1), to_outn, out_ready, (k, k + 1))

            def store(q):
                wait(act, out_ready, q * 2 + 2)
                act.dma_start(out[bass.ds(q, 1)].rearrange("o p f -> (o p) f"), outn[:, :]).then_inc(out_written, 16)

            def layer0_quarter(q, before):
                for n in range(JB):
                    round_a(q, 0, n)
                    if before is not None:
                        mlp_step(before, n, 0)
                    elif n in X_AFTER:
                        round_x(X_AFTER[n])

            def layer1_quarter(q, before):
                for n in range(JB):
                    round_a(q, 1, n)
                    if before is None:
                        mlp_step(QUARTERS - 1, n, 1)
                    else:
                        if n == ACT_COPY_AY:
                            copy_ay(before)
                        if ACT_NORM2 <= n < ACT_NORM2 + KB // 2:
                            finish(before, 2 * (n - ACT_NORM2))
                        if n == ACT_NORM2 + KB // 2:
                            store(before)

            round_x(0)
            layer0_quarter(0, None)
            act.wait_ge(params_in, 16)
            act.wait_ge(gain_ready, 1)
            act.activation(whi[:, :], par[:, 0:WM_AT], ACT.Copy).then_inc(whi_ready, 1)
            with act.Fori(1, QUARTERS) as q:
                layer0_quarter(q, q - 1)
            layer1_quarter(0, None)
            with act.Fori(1, QUARTERS - 1) as q:
                layer1_quarter(q, q - 1)
            layer1_quarter(QUARTERS - 1, QUARTERS - 2)
            last = QUARTERS - 1
            copy_ay(last)
            act.wait_ge(out_written, 16 * last)
            normalise(QUARTERS + last + 1, to_outn, out_ready, range(0, HB))
            act.wait_ge(out_ready, 2 * last + 1)
            act.dma_start(out[last][:, 0:CW], outn[:, 0:CW]).then_inc(out_written, 16)
            act.wait_ge(out_ready, 2 * last + 2)
            act.dma_start(out[last][:, CW:QW], outn[:, CW:QW]).then_inc(half_written, 16)
            act.wait_ge(out_written, 16 * QUARTERS)
            act.wait_ge(half_written, 16)

        @block.vector
        def _(dve):
            def split_x(i):
                q, k0, k1 = X_PIECES[i]
                for b in range(2):
                    dve.wait_ge(x_hi, 2 * i + b + 1)
                    dve.tensor_tensor(x_lo_parts[b][:, q, k0 * P:k1 * P], xn[:, 2 * (q % 2) + b, k0 * P:k1 * P],
                                      as_f32(x_hi_parts[b][:, q, k0 * P:k1 * P]), ALU.subtract).then_inc(x_split, 1)

            def split_a(q, layer, n):
                if layer == 0 and n == 0 and isinstance(q, int):
                    for c in range(CH):
                        dve.wait_ge((hi_half, hi_ready)[c], 1)
                        dve.tensor_tensor(alo[:, 0, c * CW:(c + 1) * CW], raw[:, 0, 0, c * CW:(c + 1) * CW],
                                          as_f32(ahi[:, 0, c * CW:(c + 1) * CW]),
                                          ALU.subtract).then_inc((lo_half, lo_ready)[c], 1)
                    return
                wait(dve, hi_ready, q * JB + (layer * QUARTERS * JB + n + 1))
                dve.tensor_tensor(alo[:, n % SPLIT, :], raw_tile(layer, n),
                                  as_f32(ahi[:, n % SPLIT, :]), ALU.subtract).then_inc(lo_ready, 1)

            def sum_rows(q, n):
                tile = raw_tile(0, n)
                if n == 1:
                    wait(dve, raw_used, q * PAIRS)
                    dve.tensor_tensor(rowsum[:, :], raw[:, 0, 0, :], tile, ALU.add).then_inc(raw_used, 1)
                elif n % 2 == 0 and n:
                    wait(dve, raw_used, q * PAIRS + n // 2)
                    dve.tensor_tensor(rowsum[:, :], rowsum[:, :], tile, ALU.add).then_inc(rowsum_step, 1)
                elif n % 2:
                    wait(dve, rowsum_step, q * (PAIRS - 1) + n // 2)
                    to = rowsum_all if n == JB - 1 else rowsum
                    dve.tensor_tensor(to[:, :], rowsum[:, :], tile, ALU.add).then_inc(raw_used, 1)

            def degrees(q):
                dve.tensor_scalar(degc[:, :], degree, 1.0, TINY, ALU.add, ALU.max).then_inc(deg_ready, 1)
                dve.tensor_scalar(degpos[:, :], degree, 1.0, 0.0, ALU.add, ALU.is_gt).then_inc(deg_ready, 1)

            def statistics(done, blocks):
                if blocks[0] == 0:
                    wait(dve, z_ready, done)
                for i in blocks:
                    dve.bn_stats(stats[:, i, :], z[:, i, :]).then_inc(stats_step, 1)

            def statistics_taken(done):
                wait(dve, stats_step, done * KB)

            def aggregate(blocks=range(KB), last=None):
                for k in blocks:
                    i = dve.bn_aggr(mv[:, k, :], stats[:, k, :])
                    if k == (blocks[-1] if last is None else last):
                        i.then_inc(stats_ready, 1)

            def residual(q):
                wait(dve, merge_done, q + 1)
                wait(dve, xb_ready, q + 1)
                wait(dve, xn_ready, q * 2)
                dve.tensor_tensor(z[:, :, :], merged, xb[:, :, :], ALU.add).then_inc(z_ready, 1)

            def mlp_step(q, n, plan):
                at, size = DVE_RESIDUAL[plan] + 1, STATISTICS[plan]
                if n == at - 1:
                    residual(q)
                if n == at:
                    degrees(q)
                if at <= n < at + KB // size:
                    statistics(q + 1, range(size * (n - at), size * (n - at + 1)))
                if n == DVE_AGGREGATE[plan]:
                    aggregate()

            def residual2(q, half, blocks, whole):
                if blocks[0] == half * HB:
                    wait(dve, project_done, q + (1 + half))
                    wait(dve, xb_ready, q + (QUARTERS + 1))
                    dve.wait_ge(xn_ready, 2 * QUARTERS)
                    wait(dve, out_ready, q * 2)
                for k in blocks:
                    i = dve.scalar_tensor_tensor(out=z[:, k, :], in0=merged[:, k, :], scalar=dcur[:, k:k + 1],
                                                 in1=xb[:, k, :], op0=ALU.mult, op1=ALU.add)
                    if k == whole:
                        i.then_inc(z_ready, 1)

            def finish_step(q, n):
                if 0 <= n - DVE_RESIDUAL2 < KB:
                    k = n - DVE_RESIDUAL2
                    residual2(q, 0, (k,), KB - 1)
                if 0 <= n - DVE_STATISTICS2 < KB // 2:
                    k = 2 * (n - DVE_STATISTICS2)
                    statistics(q + (QUARTERS + 1), (k, k + 1))
                if 0 <= n - DVE_AGGREGATE2 < 2:
                    half = n - DVE_AGGREGATE2
                    aggregate(range(half * HB, (half + 1) * HB), KB - 1)

            def layer0_quarter(q, before):
                for n in range(JB):
                    if before is not None and n == DVE_AGGREGATE[0]:
                        statistics_taken(before + 1)
                    split_a(q, 0, n)
                    sum_rows(q, n)
                    if before is not None:
                        mlp_step(before, n, 0)
                    elif X_AFTER.get(n, X_DVE) < X_DVE:
                        split_x(X_AFTER[n])

            def layer1_quarter(q, before):
                for n in range(JB):
                    if before is None and n == DVE_AGGREGATE[1]:
                        statistics_taken(QUARTERS)
                    elif before is not None and n == DVE_AGGREGATE2:
                        statistics_taken(before + (QUARTERS + 1))
                    split_a(q, 1, n)
                    if before is None:
                        mlp_step(QUARTERS - 1, n, 1)
                    else:
                        finish_step(before, n)

            split_x(0)
            layer0_quarter(0, None)
            dve.wait_ge(params_in, 16)
            dve.tensor_scalar(gain[:, :], par[:, EPS_AT:EPS_AT + 2], 1.0, 1.0, ALU.add, ALU.add).then_inc(gain_ready, 1)
            with dve.Fori(1, QUARTERS) as q:
                layer0_quarter(q, q - 1)
            layer1_quarter(0, None)
            with dve.Fori(1, QUARTERS - 1) as q:
                layer1_quarter(q, q - 1)
            layer1_quarter(QUARTERS - 1, QUARTERS - 2)
            last = QUARTERS - 1
            for half in range(2):
                blocks = range(half * KB // 2, (half + 1) * KB // 2)
                residual2(last, half, blocks, blocks[-1])
                dve.wait_ge(z_ready, QUARTERS + last + 1 + half)
                for k in blocks:
                    dve.bn_stats(stats[:, k, :], z[:, k, :]).then_inc(stats_step, 1)
                dve.wait_ge(stats_step, (QUARTERS + last) * KB + (half + 1) * KB // 2)
                aggregate(blocks)
            dve.wait_ge(norm_step, (QUARTERS + last + 1) * 3 + 2)
            dve.wait_ge(out_ready, 2 * last + 1)
            for k in blocks:
                i = dve.tensor_scalar(outn[:, k * P:(k + 1) * P], z[:, k, :], mv[:, k, 0:1], rstd[:, k:k + 1],
                                      ALU.subtract, ALU.mult)
            i.then_inc(out_ready, 1)

        @block.gpsimd
        def _(pool):
            def quarter(t, q):
                if isinstance(q, int):
                    return t[:, q, :].rearrange("p (k d) -> p k d", d=P)
                return t[:, bass.ds(q, 1), :].rearrange("p o (k d) -> p (o k) d", d=P)

            steps = [0]

            def bias_rows(at):
                return par[:, at:at + P].rearrange("p (o d) -> p o d", o=1).to_broadcast([P, KB, P])

            def split_h(q):
                for i in range(LAYERS * M):
                    wait(pool, hhi_ready, q * (LAYERS * M) + (i + 1))
                    m = i % M
                    pool.tensor_tensor(hlo[:, m, :], h[:, m, :], as_f32(hhi[:, m, :]),
                                       ALU.subtract).then_inc(hlo_ready, 1)

            def residual0(q):
                wait(pool, z_ready, q)
                pool.tensor_tensor(xb[:, :, :], as_f32(quarter(x1hi, q)), as_f32(quarter(x1lo, q)),
                                   ALU.add).then_inc(xb_step, 1)
                wait(pool, xb_step, q + 1)
                pool.tensor_tensor(xb[:, :, :], xb[:, :, :], bias_rows(BM_AT), ALU.add).then_inc(xb_ready, 1)

            def norm_factors(done, r=slice(0, KB)):
                wait(pool, stats_ready, done)
                pool.tensor_tensor(vareps[:, r], mv[:, r, 1], epsilons[:, r], ALU.add).then_inc(norm_step, 1)
                wait(pool, norm_step, (done - 1) * 3 + 1)
                pool.tensor_tensor(rstd[:, r], vareps[:, r], halves[:, r], ALU.pow).then_inc(norm_step, 1)
                wait(pool, norm_step, (done - 1) * 3 + 2)
                pool.tensor_tensor(shift[:, r], mv[:, r, 0], rstd[:, r], ALU.mult).then_inc(norm_step, 1)
                wait(pool, norm_step, (done - 1) * 3 + 3)
                pool.tensor_tensor(nshift[:, r], shift[:, r], minus[:, r], ALU.mult).then_inc(norm_ready, 1)

            def degree_factors(q):
                wait(pool, deg_ready, q * 2 + 2)
                pool.tensor_tensor(degpow[:, :], degc[:, :], halves[:, :], ALU.pow).then_inc(y_step, 1)
                wait(pool, y_step, q + 1)
                to = dall[:, q, :] if isinstance(q, int) else dall[:, bass.ds(q, 1), :].rearrange("p o k -> p (o k)")
                pool.tensor_tensor(to, degpow[:, :], degpos[:, :], ALU.mult).then_inc(y_step2, 1)

            def make_y(g, half):
                done = 2 * g + half
                r = slice(half * HB, (half + 1) * HB)
                pool.wait_ge(block_used, (QUARTERS - 1) * JB + KB * (g + 1))
                pool.wait_ge(xn_ready, done + 1)
                pool.wait_ge(y_step2, g + 1)
                if done:
                    pool.wait_ge(y_ready, done)
                d = dall[:, g, r].rearrange("p (k o) -> p k o", o=1).to_broadcast([P, HB, P])
                hi, lo = quarter(x1hi, g)[:, r, :], quarter(x1lo, g)[:, r, :]
                pool.tensor_tensor(yt[:, r, :], quarter(xn, g)[:, r, :], d, ALU.mult).then_inc(yt_ready, 1)
                if g < QUARTERS - 1:
                    pool.wait_ge(yt_ready, done + 1)
                    pool.tensor_copy(hi, yt[:, r, :]).then_inc(y_part, 1)
                    pool.wait_ge(y_part, done + 1)
                else:
                    pool.wait_ge(yhi_ready, half + 1)
                pool.tensor_tensor(lo, yt[:, r, :], as_f32(hi), ALU.subtract).then_inc(y_ready, 1)

            def add_identity(q, n):
                if n % 2 == 0:
                    wait_raw1(pool, q, n)
                k = n % KB
                square = raw_tile(1, n)[:, k * P:(k + 1) * P]
                pool.tensor_tensor(square, square, identity[:, :], ALU.add).then_inc(identity_added, 1)

            def layer1_quarter(q):
                for n in range(JB):
                    if n == POOL_NORM2:
                        norm_factors(q + QUARTERS)
                    if on_diagonal(q, n):
                        add_identity(q, n)
                prepare_layer1(q)

            def prepare_layer1(q):
                wait(pool, z_ready, q + QUARTERS)
                dq = dall[:, q, :] if isinstance(q, int) else dall[:, bass.ds(q, 1), :].rearrange("p o k -> p (o k)")
                pool.tensor_copy(dcur[:, :], dq).then_inc(xb_step, 1)
                pool.tensor_tensor(xb[:, :, :], quarter(xn, q), bias_rows(BO_AT), ALU.add).then_inc(xb_ready, 1)

            pool.memset(ones[:, :], 1.0).then_inc(const_ready, 1)
            pool.memset(halves[:, :], -0.5).then_inc(const_ready, 1)
            pool.memset(epsilons[:, :], LN_EPS).then_inc(const_ready, 1)
            pool.memset(minus[:, :], -1.0).then_inc(const_ready, 1)
            pool.memset(identity[:, :], 0.0).then_inc(const_step, 1)
            pool.wait_ge(const_step, 1)
            pool.affine_select(out=identity[:, :], in_=identity[:, :], compare_op=ALU.not_equal, fill=1.0,
                               base=0, pattern=[[-1, P]], channel_multiplier=1).then_inc(const_ready, 1)
            for i in range(X_DVE, len(X_PIECES)):
                q = X_PIECES[i][0]
                for b in range(2):
                    pool.wait_ge(x_hi, 2 * i + b + 1)
                    pool.tensor_tensor(x_lo_parts[b][:, q, :], xn[:, 2 * (q % 2) + b, :],
                                       as_f32(x_hi_parts[b][:, q, :]), ALU.subtract).then_inc(x_split2, 1)
            pool.wait_ge(const_ready, 5)
            pool.wait_ge(params_in, 16)
            pool.wait_ge(x_split, 2 * X_DVE)
            pool.wait_ge(x_split2, 2 * (len(X_PIECES) - X_DVE))
            pool.wait_ge(whi_ready, 1)
            pool.tensor_tensor(wlo[:, :], par[:, 0:WM_AT], as_f32(whi[:, :]), ALU.subtract).then_inc(wlo_ready, 1)
            with pool.Fori(0, QUARTERS - 1) as q:
                residual0(q)
                split_h(q)
                degree_factors(q)
                norm_factors(q + 1)
            residual0(QUARTERS - 1)
            for g in range(QUARTERS - 1):
                for half in range(2):
                    make_y(g, half)
                    if g == QUARTERS - 2:
                        for n in range(half * HB, (half + 1) * HB):
                            add_identity(0, n)
            degree_factors(QUARTERS - 1)
            norm_factors(QUARTERS)
            make_y(QUARTERS - 1, 0)
            make_y(QUARTERS - 1, 1)
            pool.wait_ge(y_ready, 2 * QUARTERS)
            prepare_layer1(0)
            for q in range(1, QUARTERS):
                layer1_quarter(q)
            for half in range(2):
                norm_factors(2 * QUARTERS + half, slice(half * KB // 2, (half + 1) * KB // 2))


_OUT = (N, P)


def kernel(**inputs):
    import numpy as np
    import concourse.bacc as bacc
    from concourse.bass_utils import run_bass_kernel_spmd

    x = {k: np.asarray(v) for k, v in inputs.items()}
    a = x["adj"].reshape(QUARTERS, P, KB, QUARTERS, P, KB // 2, 2)
    a_t = np.ascontiguousarray(a.transpose(0, 3, 5, 4, 6, 2, 1)).reshape(QUARTERS * PAIRS, P, 2, QW)

    def layers(w):
        return w.transpose(2, 0, 1).reshape(P, LAYERS * P)

    rows = lambda v: np.broadcast_to(v.reshape(1, -1), (P, v.size))
    params = np.ascontiguousarray(np.concatenate([
        layers(x["L0_gnn_W1"]), layers(x["L0_gnn_W2"]),
        x["L0_gnn_Wm"].reshape(P, 2, P).transpose(2, 1, 0).reshape(P, 2 * P),
        x["L1_gnn_W"].T, rows(x["L0_gnn_bm"]), rows(x["L1_gnn_b"]),
        x["L0_gnn_b1"].T, x["L0_gnn_b2"].T, rows(x["L0_gnn_eps1"]), rows(x["L0_gnn_eps2"]),
    ], axis=1))
    arrays = {
        "a_t": a_t,
        "x12": np.ascontiguousarray(np.stack([x["x"].reshape(QUARTERS, P, QW),
                                              x["L0_gnn_x2"].reshape(QUARTERS, P, QW)], axis=2)),
        "params": params,
    }
    nc = bacc.Bacc("TRN2", target_bir_lowering=False, num_devices=1)
    aps = [nc.dram_tensor(k, v.shape, F32, kind="ExternalInput").ap() for k, v in arrays.items()]
    out = nc.dram_tensor("out", (QUARTERS, P, QW), F32, kind="ExternalOutput").ap()
    build(nc, *aps, out)
    r = run_bass_kernel_spmd(nc, [arrays], core_ids=[0])
    return r.results[0]["out"].reshape(_OUT)
```
